# Optimizing a Trainium2 kernel written in Bass

```python
import numpy as np
import jax
import jax.numpy as jnp

def _softmax(x, axis=-1):
    return jax.nn.softmax(x, axis=axis)

def _gelu(x):
    return jax.nn.gelu(x, approximate=True)

def _silu(x):
    return jax.nn.silu(x)

def _sigmoid(x):
    return jax.nn.sigmoid(x)

def _layernorm(x, axis=-1, eps=1e-05):
    m = jnp.mean(x, axis=axis, keepdims=True)
    v = jnp.var(x, axis=axis, keepdims=True)
    return (x - m) / jnp.sqrt(v + eps)

def _scatter_add(tgt, idx, src, axis=0):
    return tgt.at[idx].add(src)

def _segment_sum(src, seg, n):
    return jax.ops.segment_sum(src, seg, n)
kernel_name = 'mk_perceiver_d1_seqx_r4_423291'

def setup_inputs(seed: int=0):
    np.random.seed(seed)
    _w = jnp.asarray

    def _rec_inputs():
        import jax
        import jax.numpy as jnp
        _rk = jax.random.key(seed)
        x = -0.0002928 + 1 * jax.random.normal(jax.random.fold_in(_rk, 1), (32, 64, 256), jnp.float32)
        _lenS = 64 - jax.random.randint(jax.random.fold_in(_rk, 7), (32,), 0, max(1, 64 // 4) + 1, jnp.int32)
        _lenS2 = 1601 - jax.random.randint(jax.random.fold_in(_rk, 8), (32,), 0, max(1, 1601 // 4) + 1, jnp.int32)
        _ctx_1024P = jax.random.normal(jax.random.fold_in(_rk, 11), (32, 16, 256), jnp.float32)
        _ctx_1024c = jax.random.dirichlet(jax.random.fold_in(_rk, 511), 0.3 * jnp.ones((16,), jnp.float32), (32, 1601))
        _ctx_1024t = jnp.einsum('bsk,bkd->bsd', _ctx_1024c, _ctx_1024P)
        _ctx_1024t = _ctx_1024t * jax.lax.rsqrt(jnp.mean(jnp.square(_ctx_1024t)) + 1e-12) * 0.953939
        ctx_1024 = -1.39393e-06 + 0.999914 * (_ctx_1024t + 0.3 * jax.random.normal(jax.random.fold_in(_rk, 611), (32, 1601, 256), jnp.float32))
        return (x, ctx_1024)
    x, ctx_1024 = _rec_inputs()

    def _L0_xattn_setup():
        import jax, jax.numpy as jnp
        import numpy as np
        N_HEADS = 16
        key = jax.random.key(seed)
        ks = jax.random.split(key, 8)
        B, Tq, Tkv, C = (2, 512, 512, 256)
        std = 0.02
        return {'q': jax.random.normal(ks[0], (B, Tq, C), jnp.float32), 'k': jax.random.normal(ks[1], (B, Tkv, C), jnp.float32), 'v': jax.random.normal(ks[2], (B, Tkv, C), jnp.float32), 'Wq': jax.random.normal(ks[3], (C, C), jnp.float32) * std, 'bq': jnp.zeros((C,), jnp.float32), 'Wk': jax.random.normal(ks[4], (C, C), jnp.float32) * std, 'bk': jnp.zeros((C,), jnp.float32), 'Wv': jax.random.normal(ks[5], (C, C), jnp.float32) * std, 'bv': jnp.zeros((C,), jnp.float32), 'Wo': jax.random.normal(ks[6], (C, C), jnp.float32) * std, 'bo': jnp.zeros((C,), jnp.float32)}
    _L0_xattn_all = _L0_xattn_setup()
    _L0_xattn_in = {k: v for k, v in _L0_xattn_all.items() if k in ('Wq', 'bq', 'Wk', 'bk', 'Wv', 'bv', 'Wo', 'bo')}
    del _L0_xattn_all

    def _L0_attn_setup():
        import jax, jax.numpy as jnp
        import numpy as np
        EMB = 256
        HEADS = 16
        ATT = EMB // HEADS
        key = jax.random.key(seed)
        ks = jax.random.split(key, 5)
        s = 1.0 / np.sqrt(EMB)
        return {'x': jax.random.normal(ks[0], (4, 512, EMB), dtype=jnp.float32), 'Wq': jax.random.uniform(ks[1], (EMB, HEADS * ATT), jnp.float32, -s, s), 'Wk': jax.random.uniform(ks[2], (EMB, HEADS * ATT), jnp.float32, -s, s), 'Wv': jax.random.uniform(ks[3], (EMB, HEADS * ATT), jnp.float32, -s, s), 'Wo': jax.random.uniform(ks[4], (HEADS * ATT, EMB), jnp.float32, -s, s)}
    _L0_attn_all = _L0_attn_setup()
    _L0_attn_in = {k: v for k, v in _L0_attn_all.items() if k in ('Wq', 'Wk', 'Wv', 'Wo')}
    del _L0_attn_all

    def _L0_ffn_setup():
        import math
        import jax, jax.numpy as jnp
        import numpy as np
        D_MODEL = 256
        D_HIDDEN = 512
        N_EXPERTS = 8
        TOP_K = 2
        CAPACITY_FACTOR = 1.25

        def _moe_forward(x, w_router, w_gate, w_down):
            B, T, D = x.shape
            N = B * T
            xf = x.reshape(N, D)
            logits = xf.astype(jnp.float32) @ w_router.T
            gates = jax.nn.softmax(logits, axis=-1)
            topk_gates, topk_idx = jax.lax.top_k(gates, TOP_K)
            expert_mask = jax.nn.one_hot(topk_idx, N_EXPERTS, dtype=jnp.int32).sum(axis=1)
            capacity = math.ceil(N / N_EXPERTS * CAPACITY_FACTOR)
            position_in_expert = jnp.cumsum(expert_mask, axis=0) - 1
            expert_mask = expert_mask * (position_in_expert < capacity)
            keep = jnp.take_along_axis(expert_mask, topk_idx, axis=1) > 0
            topk_gates = topk_gates * keep
            topk_gates = topk_gates / (topk_gates.sum(axis=-1, keepdims=True) + 1e-06)
            hidden = jax.nn.silu(xf @ w_gate.T)
            combine = (topk_gates[:, :, None] * jax.nn.one_hot(topk_idx, N_EXPERTS, dtype=topk_gates.dtype)).sum(axis=1)
            y = jnp.zeros((N, D), dtype=x.dtype)
            for e in range(N_EXPERTS):
                y = y + combine[:, e:e + 1] * (hidden @ w_down[e].T)
            return y.reshape(B, T, D)
        key = jax.random.key(seed)
        k0, k1, k2, k3 = jax.random.split(key, 4)
        B, T = (2, 512)
        x = jax.random.normal(k0, (B, T, D_MODEL), dtype=jnp.float32)
        w_router = jax.random.normal(k1, (N_EXPERTS, D_MODEL), dtype=jnp.float32) * 0.02
        w_gate = jax.random.normal(k2, (D_HIDDEN, D_MODEL), dtype=jnp.float32) * 0.02
        w_down = jax.random.normal(k3, (N_EXPERTS, D_MODEL, D_HIDDEN), dtype=jnp.float32) * 0.02
        return {'x': x, 'w_router': w_router, 'w_gate': w_gate, 'w_down': w_down}
    _L0_ffn_all = _L0_ffn_setup()
    _L0_ffn_in = {k: v for k, v in _L0_ffn_all.items() if k in ('w_router', 'w_gate', 'w_down')}
    del _L0_ffn_all
    return {'x': x, 'ctx_1024': ctx_1024, 'L0_xattn_Wq': _L0_xattn_in['Wq'], 'L0_xattn_bq': _L0_xattn_in['bq'], 'L0_xattn_Wk': _L0_xattn_in['Wk'], 'L0_xattn_bk': _L0_xattn_in['bk'], 'L0_xattn_Wv': _L0_xattn_in['Wv'], 'L0_xattn_bv': _L0_xattn_in['bv'], 'L0_xattn_Wo': _L0_xattn_in['Wo'], 'L0_xattn_bo': _L0_xattn_in['bo'], 'L0_attn_Wq': _L0_attn_in['Wq'], 'L0_attn_Wk': _L0_attn_in['Wk'], 'L0_attn_Wv': _L0_attn_in['Wv'], 'L0_attn_Wo': _L0_attn_in['Wo'], 'L0_ffn_w_router': _L0_ffn_in['w_router'], 'L0_ffn_w_gate': _L0_ffn_in['w_gate'], 'L0_ffn_w_down': _L0_ffn_in['w_down']}

def reference(x, ctx_1024, L0_xattn_Wq, L0_xattn_bq, L0_xattn_Wk, L0_xattn_bk, L0_xattn_Wv, L0_xattn_bv, L0_xattn_Wo, L0_xattn_bo, L0_attn_Wq, L0_attn_Wk, L0_attn_Wv, L0_attn_Wo, L0_ffn_w_router, L0_ffn_w_gate, L0_ffn_w_down):
    import jax
    import jax.numpy as jnp

    def _L0_xattn_ref(q, k, v, Wq, bq, Wk, bk, Wv, bv, Wo, bo):
        import jax, jax.numpy as jnp
        import numpy as np
        N_HEADS = 16
        b, t, c = q.shape
        h = N_HEADS
        d = c // h
        scale = d ** (-0.5)
        qh = (q @ Wq.T + bq).reshape(b, t, h, d).transpose(0, 2, 1, 3)
        kh = (k @ Wk.T + bk).reshape(b, -1, h, d).transpose(0, 2, 1, 3)
        vh = (v @ Wv.T + bv).reshape(b, -1, h, d).transpose(0, 2, 1, 3)
        attn = jnp.einsum('bhtd,bhsd->bhts', qh, kh) * scale
        attn = jax.nn.softmax(attn, axis=-1)
        out = jnp.einsum('bhts,bhsd->bhtd', attn, vh)
        out = out.transpose(0, 2, 1, 3).reshape(b, t, c)
        return out @ Wo.T + bo

    def _L0_attn_ref(x, Wq, Wk, Wv, Wo):
        import jax, jax.numpy as jnp
        import numpy as np
        EMB = 256
        HEADS = 16
        ATT = EMB // HEADS
        b, t, _ = x.shape
        h, d = (HEADS, ATT)
        scale = d ** (-0.25)
        q = (x @ Wq).reshape(b, t, h, d) * scale
        k = (x @ Wk).reshape(b, t, h, d) * scale
        v = (x @ Wv).reshape(b, t, h, d)
        dot = jnp.einsum('bqhd,bkhd->bhqk', q, k)
        causal = jnp.tril(jnp.ones((t, t), dtype=bool))
        dot = jnp.where(causal[None, None], dot, -jnp.inf)
        attn = jax.nn.softmax(dot, axis=-1)
        out = jnp.einsum('bhqk,bkhd->bqhd', attn, v).reshape(b, t, h * d)
        return out @ Wo

    def _L0_ffn_ref(x, w_router, w_gate, w_down):
        import math
        import jax, jax.numpy as jnp
        import numpy as np
        D_MODEL = 256
        D_HIDDEN = 512
        N_EXPERTS = 8
        TOP_K = 2
        CAPACITY_FACTOR = 1.25

        def _moe_forward(x, w_router, w_gate, w_down):
            B, T, D = x.shape
            N = B * T
            xf = x.reshape(N, D)
            logits = xf.astype(jnp.float32) @ w_router.T
            gates = jax.nn.softmax(logits, axis=-1)
            topk_gates, topk_idx = jax.lax.top_k(gates, TOP_K)
            expert_mask = jax.nn.one_hot(topk_idx, N_EXPERTS, dtype=jnp.int32).sum(axis=1)
            capacity = math.ceil(N / N_EXPERTS * CAPACITY_FACTOR)
            position_in_expert = jnp.cumsum(expert_mask, axis=0) - 1
            expert_mask = expert_mask * (position_in_expert < capacity)
            keep = jnp.take_along_axis(expert_mask, topk_idx, axis=1) > 0
            topk_gates = topk_gates * keep
            topk_gates = topk_gates / (topk_gates.sum(axis=-1, keepdims=True) + 1e-06)
            hidden = jax.nn.silu(xf @ w_gate.T)
            combine = (topk_gates[:, :, None] * jax.nn.one_hot(topk_idx, N_EXPERTS, dtype=topk_gates.dtype)).sum(axis=1)
            y = jnp.zeros((N, D), dtype=x.dtype)
            for e in range(N_EXPERTS):
                y = y + combine[:, e:e + 1] * (hidden @ w_down[e].T)
            return y.reshape(B, T, D)
        return _moe_forward(x, w_router, w_gate, w_down)
    x = x + _L0_xattn_ref(_layernorm(x, axis=-1), ctx_1024, ctx_1024, L0_xattn_Wq, L0_xattn_bq, L0_xattn_Wk, L0_xattn_bk, L0_xattn_Wv, L0_xattn_bv, L0_xattn_Wo, L0_xattn_bo)
    x = x + _L0_attn_ref(_layernorm(x, axis=-1), L0_attn_Wq, L0_attn_Wk, L0_attn_Wv, L0_attn_Wo)
    x = x + _L0_ffn_ref(_layernorm(x, axis=-1), L0_ffn_w_router, L0_ffn_w_gate, L0_ffn_w_down)
    return x

_drawn_inputs = setup_inputs


def setup_inputs(seed=0):
    import zlib

    import numpy as np

    out = dict(_drawn_inputs(seed))
    spreads = {'L0_xattn_bq': (0.0, 0.8),
     'L0_xattn_bk': (0.0, 0.8),
     'L0_xattn_bv': (0.0, 0.1),
     'L0_xattn_bo': (0.0, 0.1)}
    factors = {'L0_xattn_Wq': 8.0, 'L0_xattn_Wk': 8.0}
    for name, (base, spread) in spreads.items():
        noise = np.random.default_rng([zlib.crc32(name.encode()), seed]).standard_normal(out[name].shape)
        drawn = base * np.exp(spread * noise) if base else spread * noise
        out[name] = jnp.asarray(drawn.astype(out[name].dtype))
    for name, factor in factors.items():
        out[name] = (out[name] * factor).astype(out[name].dtype)
    return out
```

```python
from contextlib import ExitStack

import concourse.bass as bass
from concourse import mybir

F32 = mybir.dt.float32
F32R = mybir.dt.float32r
U32 = mybir.dt.uint32
ALU = mybir.AluOpType
ACT = mybir.ActivationFunctionType
AX = mybir.AxisListType

P = 128
B, TQ, C = 32, 64, 256
S = 1601
H, D = 16, 16
KC = C // P
HM = P // D
TILES = -(-S // P)
TAIL_ROWS = S - (TILES - 1) * P
GROUP = 4
GROUPS = -(-TILES // GROUP)
SP = S + 1
VW = D + 1
PAIRS = H // 2
BP = B // 2
E, TOPK, HID = 8, 2, 512
CAPACITY = -(-(B * TQ) * 5 // (E * 4))
KH = HID // P
EPS = 1e-5
GATE_EPS = 1e-6
NEG = -1e30
SCALE = 0.25

V_USES = -(-TILES // 2)
A_USES = 8 * (GROUPS - 1) + 2

S0, S1, PV, T = ("S0",), ("S1",), ("PV",), ("T",)


def k_(g, m):
    return ("K", g, m)


def v_(u):
    return ("V", u)


def a_(g, j):
    return ("A", g, j)


SLOTS = [
    [S0, k_(0, 0), S1, k_(0, 1), PV, T],
    [S0, a_(0, 0), S1, a_(0, 1), v_(0), PV, a_(0, 2), T],
    [S0, a_(0, 3), S1, a_(0, 4), v_(1), PV, a_(0, 5), T],
    [a_(0, 6), S0, k_(1, 0), S1, a_(0, 7), PV, k_(1, 1), T],
    [S0, a_(1, 0), S1, a_(1, 1), v_(2), PV, a_(1, 2), T],
    [S0, a_(1, 3), S1, a_(1, 4), v_(3), PV, a_(1, 5), T],
    [a_(1, 6), S0, k_(2, 0), S1, a_(1, 7), PV, k_(2, 1), T],
    [S0, a_(2, 0), S1, a_(2, 1), v_(4), PV, a_(2, 2), T],
    [S0, a_(2, 3), S1, a_(2, 4), v_(5), PV, a_(2, 5), T],
    [a_(2, 6), S0, k_(3, 0), S1, a_(2, 7), PV, k_(3, 1), T],
    [S0, a_(3, 0), S1, a_(3, 1), v_(6), PV, T],
    [S0, S1, PV, ("XT",), T],
    [S0, S1, PV, ("Q",), T],
]

YZ_ORDER = [it for slot in SLOTS for it in slot if it[0] in ("K", "A", "XT", "Q")]
YZ = {it: n % 2 for n, it in enumerate(YZ_ORDER)}
assert len(YZ_ORDER) % 2 == 0

T_PE = ["o_turned", "on_turned", "cross_out", "ln2_turned", "qk", "v", "s0", "s1", "p_turned0",
        "p_turned1", "pv", "at_turned", "self_out", "ln3_turned", "router", "cumsum", "hidden",
        "down0", "down1", "down2", "down3"]
T_DVE = ["xbo", "rden", "on", "x1", "stat2", "aggr2", "eps2", "xn2", "xnT2", "kb00", "kb01", "kb10",
         "kb11", "s0", "s1", "smax", "ssub", "ssum", "srec", "pT0", "at", "x2", "stat3",
         "aggr3", "eps3", "xn3", "xnT3", "lmax", "esum", "erec", "gates", "top8", "topi", "topf",
         "oh0", "oh1", "mask", "keep", "msum", "kept", "gk", "gsum", "geps", "grec", "comb",
         "den", "sig", "hid", "y0", "y1", "y2", "y3", "y4", "y5", "y6", "y7"]
T_ACT = ["onT0", "onT1", "qT", "vb0", "vb1", "p", "pT1", "atT", "gexp", "hexp"]
T_POOL = ["rstd2", "rstd3"]
T_SLOT = {n: k for k, n in enumerate(T_PE)}
T_DRAIN = {
    "o_turned": ("dve", "on"), "on_turned": ("act", "onT1"), "cross_out": ("dve", "x1"),
    "ln2_turned": ("dve", "xnT2"), "qk": ("dve", "kb11"), "v": ("act", "vb1"), "s0": ("dve", "s0"),
    "s1": ("dve", "s1"), "p_turned0": ("dve", "pT0"), "p_turned1": ("act", "pT1"),
    "pv": ("dve", "at"), "at_turned": ("act", "atT"), "self_out": ("dve", "x2"),
    "ln3_turned": ("dve", "xnT3"), "router": ("act", "gexp"), "cumsum": ("dve", "keep"),
    "hidden": ("dve", "hid"), "down0": ("dve", "y1"), "down1": ("dve", "y3"),
    "down2": ("dve", "y5"), "down3": ("dve", "y7"),
}


def rows_of(t):
    return P if t < TILES - 1 else TAIL_ROWS


def cols_of(g):
    return min(GROUP * P, SP - g * GROUP * P)


def build(nc, a, out):
    with ExitStack() as ctx:
        def sb(name, shape, dt=F32):
            return ctx.enter_context(nc.sbuf_tensor(name, shape, dt))

        def sem(name):
            return ctx.enter_context(nc.semaphore(name))

        ident = sb("ident", [P, P])
        ones = sb("ones", [P, P])
        ones_r = sb("ones_r", [P, P], F32R)
        tri = sb("tri", [P, P])
        head_mask = sb("head_mask", [P, HM])
        half_mask = sb("half_mask", [P, 2])
        causal = sb("causal", [P, TQ])
        iota8 = sb("iota8", [P, E])
        neg_half = sb("neg_half", [P, 1])
        wq = sb("wq", [P, KC, C])
        wo = sb("wo", [P, KC, C])
        wk_hi, wk_lo = sb("wk_hi", [P, KC, C], F32R), sb("wk_lo", [P, KC, C], F32R)
        wv_hi, wv_lo = sb("wv_hi", [P, KC, C], F32R), sb("wv_lo", [P, KC, C], F32R)
        bq, bk, bv = sb("bq", [P, KC]), sb("bk", [P, KC]), sb("bv", [P, KC])
        bo = sb("bo", [P, C])
        sq, sk, sv, so = (sb(f"s{n}", [P, KC, C]) for n in "qkvo")
        w_router = sb("w_router", [P, KC, E])
        w_gate = sb("w_gate", [P, KC, HID])
        w_down = sb("w_down", [P, KH, E * C])
        ctx_raw = [sb(f"ctx_raw{n}", [P, KC, GROUP * P]) for n in range(2)]
        ctx_hi = [sb(f"ctx_hi{n}", [P, KC, GROUP * P], F32R) for n in range(2)]
        ctx_lo = [sb(f"ctx_lo{n}", [P, KC, GROUP * P], F32R) for n in range(2)]
        k_hi = [sb(f"k_hi{n}", [P, KC, SP], F32R) for n in range(2)]
        k_lo = [sb(f"k_lo{n}", [P, KC, SP], F32R) for n in range(2)]
        v_sb = [sb(f"v_sb{n}", [P, TILES * H * VW + 2 * D]) for n in range(2)]
        probs = [sb(f"probs{n}", [P, H * TQ]) for n in range(2)]
        q_hi = [sb(f"q_hi{n}", [P, KC, HM * TQ], F32R) for n in range(2)]
        q_lo = [sb(f"q_lo{n}", [P, KC, HM * TQ], F32R) for n in range(2)]
        neg_max_diag = [sb(f"neg_max_diag{n}", [P, PAIRS, P], F32R) for n in range(2)]
        maxima = sb("maxima", [P, GROUPS, PAIRS])
        neg_max = sb("neg_max", [P, PAIRS])
        xq = [sb(f"xq{n}", [TQ, C]) for n in range(2)]
        xq_norm = sb("xq_norm", [TQ, C])
        xq_stat = sb("xq_stat", [TQ, 6])
        xq_mv = sb("xq_mv", [TQ, 4])
        xqT = sb("xqT", [P, KC, TQ])
        qT = sb("qT", [P, KC, TQ])
        qT_hi, qT_lo = sb("qT_hi", [P, KC, TQ], F32R), sb("qT_lo", [P, KC, TQ])
        o_sb = sb("o_sb", [P, 4, 2 * TQ])
        x_res = sb("x_res", [P, C])
        x_bo = x_res
        rden = sb("rden", [P, H])
        on = sb("on", [P, C])
        tT = sb("tT", [P, KC, P])
        x1, x2 = sb("x1", [P, C]), sb("x2", [P, C])
        t_stat, t_mv = sb("t_stat", [P, 6]), sb("t_mv", [P, 4])
        xn = sb("xn", [P, C])
        xnT = sb("xnT", [P, KC, P])
        sqT = sb("sqT", [P, KC, P])
        k_block = sb("k_block", [P, 2, KC, HM, TQ])
        v_block = sb("v_block", [P, 2, PAIRS, 2, D])
        s_sb = sb("s_sb", [P, H, TQ])
        flat_block = k_block[:].rearrange("p b k h t -> p (b k h t)")
        pT = flat_block[:, 0:PAIRS * P].rearrange("p (q t) -> p q t", t=P)
        hexp = flat_block[:, PAIRS * P:PAIRS * P + HID].rearrange("p (m t) -> p m t", t=P)
        hidden = flat_block[:, PAIRS * P + HID:PAIRS * P + 2 * HID].rearrange("p (m t) -> p m t", t=P)
        s_max, s_sum, s_rec = sb("s_max", [P, H]), sb("s_sum", [P, H]), sb("s_rec", [P, H])
        gate = sb("gate", [P, 12, E])
        gcol = sb("gcol", [P, 8])
        top_i = sb("top_i", [P, E], U32)
        chosen_before = sb("chosen_before", [P, E])
        y_sb = xn

        s_ps = [ctx.enter_context(nc.psum_tensor(f"s_ps{n}", [P, 2, 512], F32)) for n in range(2)]
        o_ps = ctx.enter_context(nc.psum_tensor("o_ps", [P, 512], F32))
        x_ps = ctx.enter_context(nc.psum_tensor("x_ps", [P, 512], F32))
        yz_ps = [ctx.enter_context(nc.psum_tensor(f"yz_ps{n}", [P, 512], F32)) for n in range(2)]

        weights_in = sem("weights_in")
        tail_weights_in = sem("tail_weights_in")
        consts_ready = sem("consts_ready")
        split_ready = sem("split_ready")
        ctx_in = [sem(f"ctx_in{n}") for n in range(2)]
        xq_in = [sem(f"xq_in{n}") for n in range(2)]
        res_in = sem("res_in")
        out_done = sem("out_done")
        wait_carrier = sem("wait_carrier")
        ctx_hi_made = sem("ctx_hi_made")
        ctx_cut = sem("ctx_cut")
        k_filled, k_hi_made, k_lo_made = sem("k_filled"), sem("k_hi_made"), sem("k_lo_made")
        v_filled, v_copied = sem("v_filled"), sem("v_copied")
        a_filled, a_reduced = sem("a_filled"), sem("a_reduced")
        neg_max_made = sem("neg_max_made")
        bias_ready = sem("bias_ready")
        q_filled, q_drained = sem("q_filled"), sem("q_drained")
        q_norm_step = sem("q_norm_step")
        q_rstd = sem("q_rstd")
        q_cut_step = sem("q_cut_step")
        scores_ready, probs_ready, pv_done = sem("scores_ready"), sem("probs_ready"), sem("pv_done")
        o_copied = sem("o_copied")
        t_pe, t_dve, t_act, t_pool = sem("t_pe"), sem("t_dve"), sem("t_act"), sem("t_pool")

        def apart(eng):
            eng.sem_inc(wait_carrier, 1)

        def tail_wait(eng, who, name, p):
            s, names = {"pe": (t_pe, T_PE), "dve": (t_dve, T_DVE), "act": (t_act, T_ACT),
                        "pool": (t_pool, T_POOL)}[who]
            eng.wait_ge(s, p * len(names) + names.index(name) + 1)

        N_CONST, N_SPLIT, N_WEIGHTS, N_TAIL_WEIGHTS = 13, 7, 7, 8

        block = ctx.enter_context(nc.Block())

        def run(eng, step, tail_only, begin):
            begin()
            step(eng, -2, 0, None, main=False, prep=False, qprep=True, tail=False)
            step(eng, -1, 1, None, main=False, prep=True, qprep=True, tail=False)
            step(eng, 0, 0, 0, main=True, prep=True, qprep=True, tail=False)
            step(eng, 1, 1, 0, main=True, prep=True, qprep=True, tail=False)
            with eng.Fori(1, BP - 1) as i:
                step(eng, i * 2, 0, i, main=True, prep=True, qprep=True, tail=True)
                step(eng, i * 2 + 1, 1, i, main=True, prep=True, qprep=True, tail=True)
            step(eng, B - 2, 0, BP - 1, main=True, prep=True, qprep=False, tail=True)
            step(eng, B - 1, 1, BP - 1, main=True, prep=False, qprep=False, tail=True)
            tail_only(BP - 1)

        def pieces():
            return [(t, it) for t in range(TILES) for it in SLOTS[t]]

        def tail_of_slot(c, t):
            k = c * TILES + t
            return [n for n in T_PE if T_SLOT[n] == k]

        xr = a["x"].rearrange("b t d -> (b t) d")
        outr = out.rearrange("b t d -> (b t) d")
        ctx_t = a["ctx_t"]

        @block.sync
        def _(sp):
            def begin():
                def load(dst, src):
                    sp.dma_start(dst, src).then_inc(weights_in, 16)
                sp.sem_inc(out_done, 16)
                load(wq[:], a["wq"].rearrange("(k p) n -> p k n", p=P))
                load(staged[0], a["wk"].rearrange("(k p) n -> p k n", p=P))
                load(staged[1], a["wv"].rearrange("(k p) n -> p k n", p=P))
                for dst, n in ((bq, "bq"), (bk, "bk"), (bv, "bv")):
                    load(dst[:], a[n])
                load(bo[:], a["bo"].partition_broadcast(P))

            def late_weights():
                for dst, n in ((wo, "wo"), (sq, "sq"), (sk, "sk"), (sv, "sv"), (so, "so"),
                               (w_router, "router"), (w_gate, "gate"), (w_down, "down")):
                    sp.dma_start(dst[:], a[n].rearrange("(k p) n -> p k n", p=P)).then_inc(tail_weights_in, 16)

            def step(sp, b, c, i, main, prep, qprep, tail):
                if qprep:
                    if main:
                        sp.wait_ge(q_norm_step, b * 4 + 4)
                    sp.dma_start(xq[c][:], xr[bass.ds(b * TQ + 2 * TQ, TQ), :]).then_inc(xq_in[c], 16)
                if tail and c == 0:
                    load_res(sp, i - 1)
                for gr in range(GROUPS) if qprep else ():
                    if gr == 2:
                        if not main and prep:
                            late_weights()
                        if tail and c == 1:
                            store(sp, i - 1)
                    load_ctx(sp, b + 2, gr)
                if tail and c == 1 and not qprep:
                    store(sp, i - 1)

            def load_ctx(sp, b, gr):
                if not (isinstance(b, int) and b == 0 and gr < 2):
                    sp.wait_ge(ctx_cut, b * GROUPS + gr - 1)
                n = min(GROUP * P, S - gr * GROUP * P)
                sp.dma_start(ctx_raw[gr % 2][:, :, 0:n],
                             ctx_t[bass.ds(b * C, C), gr * GROUP * P:gr * GROUP * P + n]
                             .rearrange("(k p) s -> p k s", p=P)).then_inc(ctx_in[gr % 2], 16)

            def load_res(sp, p):
                sp.dma_start(x_res[:], xr[bass.ds(p * P, P), :]).then_inc(res_in, 16)

            def store(sp, p):
                tail_wait(sp, "dve", "y7", p)
                sp.dma_start(outr[bass.ds(p * P, P), :], y_sb[:]).then_inc(out_done, 16)

            def tail_only(p):
                load_res(sp, p)
                store(sp, p)
                sp.wait_ge(out_done, 16 * BP + 16)

            staged = [hidden[:].rearrange("p (k x) n -> p k (x n)", k=KC),
                      hexp[:].rearrange("p (k x) n -> p k (x n)", k=KC)]
            run(sp, step, tail_only, begin)

        @block.gpsimd
        def _(pool):
            g = nc.gpsimd

            def begin():
                n = [0]

                def made(ins):
                    n[0] += 1
                    ins.then_inc(consts_ready, 1)
                    pool.wait_ge(consts_ready, n[0])

                made(g.memset(ones[:], 1.0))
                made(g.affine_select(out=ident[:], in_=ones[:], compare_op=ALU.is_equal, fill=0.0, base=0,
                                     pattern=[[-1, P]], channel_multiplier=1))
                made(g.affine_select(out=tri[:], in_=ones[:], compare_op=ALU.is_ge, fill=0.0, base=0,
                                     pattern=[[1, P]], channel_multiplier=-1))
                made(g.affine_select(out=head_mask[:], in_=ones[:, 0:HM], compare_op=ALU.is_ge, fill=0.0,
                                     base=0, pattern=[[-D, HM]], channel_multiplier=1))
                made(g.affine_select(out=head_mask[:], in_=head_mask[:], compare_op=ALU.is_ge, fill=0.0,
                                     base=D - 1, pattern=[[D, HM]], channel_multiplier=-1))
                made(g.affine_select(out=half_mask[:], in_=ones[:, 0:2], compare_op=ALU.is_ge, fill=0.0,
                                     base=0, pattern=[[-TQ, 2]], channel_multiplier=1))
                made(g.affine_select(out=half_mask[:], in_=half_mask[:], compare_op=ALU.is_ge, fill=0.0,
                                     base=TQ - 1, pattern=[[TQ, 2]], channel_multiplier=-1))
                made(g.memset(causal[:], 0.0))
                for lo in (0, TQ):
                    made(g.affine_select(out=causal[lo:lo + TQ, :], in_=causal[lo:lo + TQ, :],
                                         compare_op=ALU.is_ge, fill=NEG, base=0, pattern=[[-1, TQ]],
                                         channel_multiplier=1))
                made(g.iota(iota8[:], pattern=[[1, E]], base=0, channel_multiplier=0,
                            allow_small_or_imprecise_dtypes=True))
                made(g.memset(neg_half[:], -0.5))
                made(g.memset(chosen_before[:], 0.0))

            def cut_q(b, c):
                v = b * 4
                pool.wait_ge(q_drained, b * 2 + 2)
                if not (isinstance(b, int) and b == 0):
                    pool.wait_ge(q_cut_step, v)
                apart(pool)
                g.tensor_copy(qT_hi[:], qT[:]).then_inc(q_cut_step, 1)
                pool.wait_ge(q_cut_step, v + 1)
                g.tensor_tensor(qT_lo[:], qT[:], qT_hi[:].bitcast(F32), ALU.subtract).then_inc(q_cut_step, 1)
                pool.wait_ge(q_cut_step, v + 2)
                shape = [P, KC, HM, TQ]
                mask = head_mask[:].unsqueeze(2).unsqueeze(1).to_broadcast(shape)
                for src, dst in ((qT_hi[:].bitcast(F32), q_hi[c]), (qT_lo[:], q_lo[c])):
                    g.tensor_tensor(dst[:].rearrange("p k (h t) -> p k h t", t=TQ),
                                    src.unsqueeze(2).to_broadcast(shape), mask,
                                    ALU.mult).then_inc(q_cut_step, 1)

            def cut_ctx(b, c, gr):
                n = cols_of(gr)
                pool.wait_ge(ctx_in[gr % 2], b * 32 + (gr // 2) * 16 + 16)
                if gr >= 2:
                    pool.wait_ge(v_filled, b * V_USES + 2 * gr - 2)
                elif not (isinstance(b, int) and b == 0):
                    pool.wait_ge(v_filled, b * V_USES - 1 + gr)
                src = ctx_raw[gr % 2][:, :, 0:n]
                hi, lo = ctx_hi[gr % 2][:, :, 0:n], ctx_lo[gr % 2][:, :, 0:n]
                apart(pool)
                g.tensor_copy(hi, src).then_inc(ctx_hi_made, 1)
                pool.wait_ge(ctx_hi_made, b * GROUPS + gr + 1)
                g.tensor_tensor(lo, src, hi.bitcast(F32), ALU.subtract).then_inc(ctx_cut, 1)

            def rstd(s, mv, p):
                g.tensor_tensor(mv[:, 3:4], mv[:, 2:3], neg_half[0:p, :], ALU.pow).then_inc(s, 1)

            def step(pool, b, c, i, main, prep, qprep, tail):
                if prep:
                    if main and not (isinstance(b, int) and b == 0):
                        pool.wait_ge(scores_ready, b * TILES)
                    cut_q(b + 1, 1 - c)
                for t in range(TILES):
                    if prep and t in (3, 6):
                        cut_ctx(b + 1, 1 - c, t // 3 + 1)
                    if qprep and t in (9, 11):
                        cut_ctx(b + 2, c, (t - 9) // 2)
                    if qprep and t == 10:
                        pool.wait_ge(q_norm_step, b * 4 + 11)
                        rstd(q_rstd, xq_mv, TQ)
                    if tail:
                        for n in tail_of_slot(c, t):
                            tail_part(n, i - 1)

            def tail_part(n, p):
                if n in ("cross_out", "self_out"):
                    k = "2" if n == "cross_out" else "3"
                    tail_wait(pool, "dve", "eps" + k, p)
                    rstd(t_pool, t_mv, P)

            def tail_only(p):
                for n in T_PE:
                    tail_part(n, p)

            run(pool, step, tail_only, begin)

        @block.scalar
        def _(act):
            s = nc.scalar

            def begin():
                pass

            def exp_tile(b, c, t):
                par, r = (c + t) % 2, rows_of(t)
                act.wait_ge(scores_ready, b * TILES + t + 1)
                if not (isinstance(b, int) and b == 0 and t < 2):
                    act.wait_ge(pv_done, b * TILES + t - 1)
                s.activation(probs[par][0:r, :], s_ps[par][0:r].rearrange("p a n -> p (a n)"),
                             ACT.Exp).then_inc(probs_ready, 1)

            def k_part(b, c, gr, m):
                n = cols_of(gr)
                act.wait_ge(k_filled, b * 8 + gr * 2 + m + 1)
                s.activation(k_hi[c][:, m, gr * GROUP * P:gr * GROUP * P + n],
                             yz_ps[YZ[("K", gr, m)]][:, 0:n], ACT.Identity,
                             bias=bk[:, m:m + 1]).then_inc(k_hi_made, 1)

            def v_part(b, c, u):
                act.wait_ge(v_filled, b * V_USES + u + 1)
                n = 2 if 2 * u + 1 < TILES else 1
                r = rows_of(2 * u)
                dst = v_sb[c][0:r, 2 * u * H * VW:(2 * u + n) * H * VW].rearrange("p (h d) -> p h d", d=VW)
                src = x_ps[0:r, 0:n * C].rearrange("p (h d) -> p h d", d=D)
                s.activation(dst[:, :, 0:D], src, ACT.Copy).then_inc(v_copied, 1)

            def tail_part(n, p):
                if n not in ("on_turned", "qk", "v", "s1", "p_turned1", "at_turned", "router", "hidden"):
                    return
                tail_wait(act, "pe", n, p)
                if n == "on_turned":
                    for k in range(KC):
                        s.activation(tT[:, k, :], x_ps[:, k * P:(k + 1) * P], ACT.Identity,
                                     bias=bv[:, k:k + 1]).then_inc(t_act, 1)
                elif n == "qk":
                    s.activation(sqT[:].rearrange("p k t -> p (k t)"), x_ps[:, 0:KC * P], ACT.Copy,
                                 scale=SCALE).then_inc(t_act, 1)
                elif n == "v":
                    src = x_ps[:].rearrange("p (b q h d) -> p (b q) h d", b=2, q=PAIRS, h=2)
                    for h in range(2):
                        dst = v_block[:].rearrange("p b q h d -> p (b q) h d")
                        s.activation(dst[:, :, h, :], src[:, :, h, :], ACT.Copy,
                                     scale=half_mask[:, h:h + 1]).then_inc(t_act, 1)
                elif n == "s1":
                    tail_wait(act, "dve", "ssub", p)
                    s.activation(s_sb[:], s_sb[:], ACT.Exp).then_inc(t_act, 1)
                elif n == "p_turned1":
                    s.activation(pT[:, 4:8, :], x_ps[:].rearrange("p (q t) -> p q t", q=4),
                                 ACT.Copy).then_inc(t_act, 1)
                elif n == "at_turned":
                    s.activation(tT[:], x_ps[:, 0:KC * P].rearrange("p (k t) -> p k t", k=KC),
                                 ACT.Copy).then_inc(t_act, 1)
                elif n == "router":
                    tail_wait(act, "dve", "lmax", p)
                    s.activation(gate[:, 0, :], x_ps[:, 0:E], ACT.Exp, bias=gcol[:, 0:1]).then_inc(t_act, 1)
                elif n == "hidden":
                    s.activation(hexp[:].rearrange("p m t -> p (m t)"), x_ps[:], ACT.Exp,
                                 scale=-1.0).then_inc(t_act, 1)

            def step(act, b, c, i, main, prep, qprep, tail):
                if not main and not prep:
                    act.wait_ge(weights_in, 16 * N_WEIGHTS)
                    act.wait_ge(consts_ready, N_CONST)
                for t, it in pieces():
                    if it == S1 and main:
                        exp_tile(b, c, t)
                    elif it[0] == "K" and prep:
                        k_part(b + 1, 1 - c, it[1], it[2])
                    elif it[0] == "V" and prep:
                        if it[1] == 0 and not main:
                            act.wait_ge(split_ready, N_SPLIT)
                        v_part(b + 1, 1 - c, it[1])
                    elif it == T and tail:
                        for n in tail_of_slot(c, t):
                            tail_part(n, i - 1)

            def tail_only(p):
                for n in T_PE:
                    tail_part(n, p)

            run(act, step, tail_only, begin)

        @block.vector
        def _(dve):
            v = nc.vector

            def begin():
                n = [0]

                def made(ins):
                    n[0] += 1
                    ins.then_inc(split_ready, 1)
                    dve.wait_ge(split_ready, n[0])

                made(v.memset(v_sb[0][:], 1.0))
                made(v.memset(v_sb[1][:], 1.0))
                dve.wait_ge(consts_ready, N_CONST)
                made(v.tensor_copy(ones_r[:], ones[:]))
                dve.wait_ge(weights_in, 16 * N_WEIGHTS)
                for src, hi, lo in ((hidden, wk_hi, wk_lo), (hexp, wv_hi, wv_lo)):
                    src = src[:].rearrange("p (k x) n -> p k (x n)", k=KC)
                    made(v.tensor_copy(hi[:], src))
                    made(v.tensor_tensor(lo[:], src, hi[:].bitcast(F32), ALU.subtract))

            def k_part(b, c, gr, m):
                n = cols_of(gr)
                cols = slice(gr * GROUP * P, gr * GROUP * P + n)
                dve.wait_ge(k_hi_made, b * 8 + gr * 2 + m + 1)
                v.scalar_tensor_tensor(out=k_lo[c][:, m, cols], in0=yz_ps[YZ[("K", gr, m)]][:, 0:n],
                                       scalar=bk[:, m:m + 1], in1=k_hi[c][:, m, cols].bitcast(F32),
                                       op0=ALU.add, op1=ALU.subtract).then_inc(k_lo_made, 1)

            def a_part(b, c, gr, j):
                n = 8 * gr + j
                dve.wait_ge(a_filled, b * A_USES + n + 1)
                ps = yz_ps[YZ[("A", gr, j)]]
                if gr < GROUPS - 1:
                    v.tensor_reduce(maxima[:, gr, j:j + 1], ps[:, 0:GROUP * P], AX.X,
                                    ALU.max).then_inc(a_reduced, 1)
                else:
                    w = cols_of(gr)
                    src = ps[:, 0:4 * w].rearrange("p (q n) -> p q n", q=4)[:, :, 0:TAIL_ROWS]
                    v.tensor_reduce(maxima[:, gr, 4 * j:4 * j + 4], src, AX.X,
                                    ALU.max).then_inc(a_reduced, 1)

            def max_part(b, c):
                dve.wait_ge(a_reduced, b * A_USES + A_USES)
                v.tensor_reduce(neg_max[:], maxima[:].rearrange("p g q -> p q g"), AX.X, ALU.max,
                                negate=True).then_inc(neg_max_made, 1)
                dve.wait_ge(neg_max_made, b + 1)
                v.tensor_tensor(neg_max_diag[c][:], ident[:].unsqueeze(1).to_broadcast([P, PAIRS, P]),
                                neg_max[:].unsqueeze(2).to_broadcast([P, PAIRS, P]),
                                ALU.mult).then_inc(bias_ready, 1)

            def norm_stats(b, c):
                dve.wait_ge(xq_in[c], (b - c) * 8 + 16)
                v.bn_stats(xq_stat[:], xq[c][:]).then_inc(q_norm_step, 1)
                dve.wait_ge(q_norm_step, b * 4 + 1)
                apart(dve)
                v.bn_aggr(xq_mv[:, 0:2], xq_stat[:]).then_inc(q_norm_step, 1)
                dve.wait_ge(q_norm_step, b * 4 + 2)
                v.tensor_scalar(xq_mv[:, 2:3], xq_mv[:, 1:2], EPS, None, ALU.add).then_inc(q_norm_step, 1)

            def norm_apply(b, c):
                dve.wait_ge(q_rstd, b + 1)
                v.tensor_scalar(xq_norm[:], xq[c][:], xq_mv[:, 0:1], xq_mv[:, 3:4], ALU.subtract,
                                ALU.mult).then_inc(q_norm_step, 1)

            def xt_part(b):
                dve.wait_ge(q_filled, b * 2 + 1)
                v.tensor_copy(xqT[:].rearrange("p k t -> p (k t)"),
                              yz_ps[YZ[("XT",)]][:, 0:KC * TQ]).then_inc(q_drained, 1)

            def q_part(b):
                dve.wait_ge(q_filled, b * 2 + 2)
                if not (isinstance(b, int) and b == 0):
                    dve.wait_ge(q_cut_step, b * 4)
                for m in range(KC):
                    ins = v.tensor_scalar(qT[:, m, :], yz_ps[YZ[("Q",)]][:, m * TQ:(m + 1) * TQ],
                                          bq[:, m:m + 1], SCALE, ALU.add, ALU.mult)
                ins.then_inc(q_drained, 1)

            def copy_o(b, c, i):
                dve.wait_ge(pv_done, b * TILES + TILES)
                src = o_ps[:, 0:4 * TQ].rearrange("p (g t) -> p g t", g=4)
                v.tensor_copy(o_sb[:, :, c * TQ:(c + 1) * TQ], src).then_inc(o_copied, 1)

            def bcast(ap, shape, axis):
                return ap.unsqueeze(axis).to_broadcast(shape)

            def tail_part(n, p):
                def done(ins, name):
                    ins.then_inc(t_dve, 1)
                    tail_wait(dve, "dve", name, p)

                def norm(x, k):
                    done(v.bn_stats(t_stat[:], x[:]), "stat" + k)
                    apart(dve)
                    done(v.bn_aggr(t_mv[:, 0:2], t_stat[:]), "aggr" + k)
                    done(v.tensor_scalar(t_mv[:, 2:3], t_mv[:, 1:2], EPS, None, ALU.add), "eps" + k)
                    tail_wait(dve, "pool", "rstd" + k, p)
                    done(v.tensor_scalar(xn[:], x[:], t_mv[:, 0:1], t_mv[:, 3:4], ALU.subtract, ALU.mult),
                         "xn" + k)

                if n in T_DRAIN and n not in ("on_turned", "v", "p_turned1", "at_turned"):
                    tail_wait(dve, "pe", n, p)
                if n == "o_turned":
                    dve.wait_ge(res_in, p * 16 + 16)
                    done(v.tensor_tensor(x_bo[:], x_res[:], bo[:], ALU.add), "xbo")
                    o = x_ps[:].rearrange("p (h d) -> p h d", d=2 * D)
                    done(v.reciprocal(rden[:].unsqueeze(2), o[:, :, D:D + 1]), "rden")
                    done(v.tensor_tensor(on[:].rearrange("p (h d) -> p h d", d=D), o[:, :, 0:D],
                                         bcast(rden[:], [P, H, D], 2), ALU.mult), "on")
                elif n == "cross_out":
                    done(v.tensor_tensor(x1[:], x_ps[:, 0:C], x_bo[:], ALU.add), "x1")
                    dve.wait_ge(out_done, p * 16 + 16)
                    norm(x1, "2")
                elif n in ("ln2_turned", "ln3_turned"):
                    done(v.tensor_copy(xnT[:].rearrange("p k t -> p (k t)"), x_ps[:, 0:KC * P]),
                         "xnT" + n[2])
                elif n == "qk":
                    tail_wait(dve, "act", "qT", p)
                    for bb in range(2):
                        for m in range(KC):
                            src = x_ps[:, (KC + m) * P + bb * TQ:(KC + m) * P + (bb + 1) * TQ]
                            done(v.tensor_tensor(k_block[:, bb, m], bcast(src, [P, HM, TQ], 1),
                                                 bcast(head_mask[:], [P, HM, TQ], 2), ALU.mult),
                                 f"kb{bb}{m}")
                elif n in ("s0", "s1"):
                    m = int(n[1])
                    done(v.tensor_tensor(s_sb[:, m * HM:(m + 1) * HM, :],
                                         x_ps[:].rearrange("p (h t) -> p h t", t=TQ),
                                         bcast(causal[:], [P, HM, TQ], 1), ALU.add), n)
                    if m == 1:
                        done(v.tensor_reduce(s_max[:], s_sb[:], AX.X, ALU.max), "smax")
                        done(v.tensor_tensor(s_sb[:], s_sb[:], bcast(s_max[:], [P, H, TQ], 2),
                                             ALU.subtract), "ssub")
                        tail_wait(dve, "act", "p", p)
                        done(v.tensor_reduce(s_sum[:], s_sb[:], AX.X, ALU.add), "ssum")
                        done(v.reciprocal(s_rec[:], s_sum[:]), "srec")
                elif n == "p_turned0":
                    done(v.tensor_copy(pT[:, 0:4, :], x_ps[:].rearrange("p (q t) -> p q t", q=4)), "pT0")
                elif n == "pv":
                    done(v.tensor_tensor(on[:].rearrange("p (h d) -> p h d", d=D),
                                         x_ps[:, 0:C].rearrange("p (h d) -> p h d", d=D),
                                         bcast(s_rec[:], [P, H, D], 2), ALU.mult), "at")
                elif n == "self_out":
                    done(v.tensor_tensor(x2[:], x_ps[:, 0:C], x1[:], ALU.add), "x2")
                    norm(x2, "3")
                elif n == "router":
                    done(v.tensor_reduce(gcol[:, 0:1], x_ps[:, 0:E], AX.X, ALU.max, negate=True), "lmax")
                    tail_wait(dve, "act", "gexp", p)
                    done(v.tensor_reduce(gcol[:, 1:2], gate[:, 0, :], AX.X, ALU.add), "esum")
                    done(v.reciprocal(gcol[:, 2:3], gcol[:, 1:2]), "erec")
                    done(v.tensor_scalar(gate[:, 1, :], gate[:, 0, :], gcol[:, 2:3], None, ALU.mult), "gates")
                    apart(dve)
                    done(v.max(gate[:, 2, :], gate[:, 1, :]), "top8")
                    apart(dve)
                    done(v.max_index(top_i[:], gate[:, 2, :], gate[:, 1, :]), "topi")
                    done(v.tensor_copy(gate[:, 3, :], top_i[:]), "topf")
                    for k in range(TOPK):
                        done(v.tensor_scalar(gate[:, 4 + k, :], iota8[:], gate[:, 3, k:k + 1], None,
                                             ALU.is_equal), f"oh{k}")
                    done(v.tensor_tensor(gate[:, 6, :], gate[:, 4, :], gate[:, 5, :], ALU.add), "mask")
                elif n == "cumsum":
                    done(v.tensor_scalar(gate[:, 7, :], x_ps[:, 0:E], float(CAPACITY), None, ALU.is_le),
                         "keep")
                    done(v.tensor_tensor(chosen_before[:], chosen_before[:], gate[:, 6, :], ALU.add), "msum")
                    done(v.tensor_tensor(gate[:, 8, :], gate[:, 6, :], gate[:, 7, :], ALU.mult), "kept")
                    done(v.tensor_tensor(gate[:, 9, :], gate[:, 8, :], gate[:, 1, :], ALU.mult), "gk")
                    done(v.tensor_reduce(gcol[:, 3:4], gate[:, 9, :], AX.X, ALU.add), "gsum")
                    done(v.tensor_scalar(gcol[:, 4:5], gcol[:, 3:4], GATE_EPS, None, ALU.add), "geps")
                    done(v.reciprocal(gcol[:, 5:6], gcol[:, 4:5]), "grec")
                    done(v.tensor_scalar(gate[:, 10, :], gate[:, 9, :], gcol[:, 5:6], None, ALU.mult), "comb")
                elif n == "hidden":
                    he, hi = (z[:].rearrange("p m t -> p (m t)") for z in (hexp, hidden))
                    tail_wait(dve, "act", "hexp", p)
                    done(v.tensor_scalar(he, he, 1.0, None, ALU.add), "den")
                    done(v.reciprocal(he, he), "sig")
                    done(v.tensor_tensor(hi, x_ps[:], he, ALU.mult), "hid")
                elif n.startswith("down"):
                    for k in range(2):
                        e = 2 * int(n[4]) + k
                        done(v.scalar_tensor_tensor(out=y_sb[:], in0=x_ps[:, k * C:(k + 1) * C],
                                                    scalar=gate[:, 10, e:e + 1],
                                                    in1=(x2 if e == 0 else y_sb)[:], op0=ALU.mult,
                                                    op1=ALU.add), f"y{e}")

            def step(dve, b, c, i, main, prep, qprep, tail):
                for t, it in pieces():
                    if it[0] == "K" and prep:
                        k_part(b + 1, 1 - c, it[1], it[2])
                    elif it[0] == "A" and prep:
                        a_part(b + 1, 1 - c, it[1], it[2])
                        if it == a_(GROUPS - 1, 1):
                            max_part(b + 1, 1 - c)
                    elif it == PV and qprep and t == 9:
                        norm_stats(b + 2, c)
                    elif it == PV and qprep and t == 10:
                        norm_apply(b + 2, c)
                    elif it[0] == "XT" and qprep:
                        xt_part(b + 2)
                    elif it[0] == "Q" and qprep:
                        q_part(b + 2)
                    elif it == T and tail:
                        for n in tail_of_slot(c, t):
                            tail_part(n, i - 1)
                if main:
                    if c == 0 and not (isinstance(i, int) and i == 0):
                        tail_wait(dve, "pe", "o_turned", i - 1)
                    copy_o(b, c, i)

            def tail_only(p):
                for n in T_PE:
                    tail_part(n, p)

            run(dve, step, tail_only, begin)

        @block.tensor
        def _(pe):
            mm, tr = nc.tensor.matmul, nc.tensor.transpose
            last_x = [None]

            def x_free():
                if last_x[0] is not None:
                    last_x[0]()

            def yz_free(it, b):
                n = YZ_ORDER.index(it)
                if isinstance(b, int) and b == -2:
                    return
                if n < 2:
                    pe.wait_ge(q_drained, b * 2 + n + 3)
                elif YZ_ORDER[n - 2][0] == "K":
                    _, gr, m = YZ_ORDER[n - 2]
                    pe.wait_ge(k_lo_made, b * 8 + gr * 2 + m + 9)
                else:
                    _, gr, j = YZ_ORDER[n - 2]
                    pe.wait_ge(a_reduced, b * A_USES + A_USES + gr * 8 + j + 1)

            def three(out_, wt_hi, wt_lo, mv_hi, mv_lo):
                n = 0
                for k in range(KC):
                    for w_, m_ in ((wt_hi, mv_hi), (wt_hi, mv_lo), (wt_lo, mv_hi)):
                        ins = mm(out_, w_[:, k], m_[:, k], start=(n == 0), stop=(n == 3 * KC - 1))
                        n += 1
                return ins

            def full(out_, w_, m_, chunks):
                for k in range(chunks):
                    ins = mm(out_, w_(k), m_(k), start=(k == 0), stop=(k == chunks - 1))
                return ins

            def k_part(b, gr, m):
                n, cols = cols_of(gr), slice(m * P, (m + 1) * P)
                if m == 0:
                    pe.wait_ge(ctx_cut, b * GROUPS + gr + 1)
                ch, cl = ctx_hi[gr % 2][:, :, 0:n], ctx_lo[gr % 2][:, :, 0:n]
                three(yz_ps[YZ[("K", gr, m)]][:, 0:n], wk_hi[:, :, cols], wk_lo[:, :, cols], ch,
                      cl).then_inc(k_filled, 1)

            def v_part(b, u):
                x_free()
                for t in range(2 * u, min(2 * u + 2, TILES)):
                    gr, r = t // GROUP, rows_of(t)
                    cols = slice((t % GROUP) * P, (t % GROUP) * P + r)
                    ins = three(x_ps[0:r, (t % 2) * C:(t % 2 + 1) * C], ctx_hi[gr % 2][:, :, cols],
                                ctx_lo[gr % 2][:, :, cols], wv_hi[:], wv_lo[:])
                ins.then_inc(v_filled, 1)
                last_x[0] = lambda: pe.wait_ge(v_copied, b * V_USES + u + 1)

            def a_part(b, c, gr, j):
                if gr == 0 and j == 0:
                    pe.wait_ge(q_cut_step, b * 4 + 4)
                if j == 0:
                    pe.wait_ge(k_hi_made, b * 8 + gr * 2 + 2)
                n = cols_of(gr)
                cols = slice(gr * GROUP * P, gr * GROUP * P + n)
                ps = yz_ps[YZ[("A", gr, j)]]
                pairs = [j] if gr < GROUPS - 1 else range(4 * j, 4 * j + 4)
                for k, q in enumerate(pairs):
                    m, h = q // 4, 2 * (q % 4)
                    ins = mm(ps[:, k * n:(k + 1) * n], q_hi[c][:, m, h * TQ:(h + 2) * TQ], k_hi[c][:, m, cols],
                             start=True, stop=True)
                ins.then_inc(a_filled, 1)

            def scores(b, c, t, m):
                par, r = (c + t) % 2, rows_of(t)
                if m == 0:
                    if t == 0:
                        pe.wait_ge(bias_ready, b + 1)
                        pe.wait_ge(k_lo_made, b * 8 + 8)
                    if not (isinstance(b, int) and b == 0 and t < 2):
                        pe.wait_ge(probs_ready, b * TILES + t - 1)
                cols = slice(t * P, t * P + r)
                o = s_ps[par][0:r, m, :]
                mm(o, ones_r[:, 0:r], neg_max_diag[c][:, 4 * m:4 * m + 4, :].rearrange("p q n -> p (q n)"),
                   start=True, stop=False)
                qh, ql = q_hi[c][:, m], q_lo[c][:, m]
                mm(o, k_hi[c][:, m, cols], qh, start=False, stop=False)
                mm(o, k_hi[c][:, m, cols], ql, start=False, stop=False)
                ins = mm(o, k_lo[c][:, m, cols], qh, start=False, stop=True)
                if m == KC - 1:
                    ins.then_inc(scores_ready, 1)

            def pv(b, c, t):
                par, r = (c + t) % 2, rows_of(t)
                pe.wait_ge(probs_ready, b * TILES + t + 1)
                if t == 0:
                    pe.wait_ge(v_copied, b * V_USES + V_USES)
                    if not (isinstance(b, int) and b == 0):
                        pe.wait_ge(o_copied, b)
                for gr in range(4):
                    for j in range(4):
                        h = 4 * gr + j
                        off = (t * H + h) * VW
                        ins = mm(o_ps[32 * j:32 * j + 32, gr * TQ:(gr + 1) * TQ],
                                 v_sb[c][0:r, off:off + 32], probs[par][0:r, h * TQ:(h + 1) * TQ],
                                 start=(t == 0 and gr == 0), stop=(t == TILES - 1 and gr == 3),
                                 skip_group_check=True)
                ins.then_inc(pv_done, 1)

            def xt_part(b):
                pe.wait_ge(q_norm_step, b * 4 + 4)
                apart(pe)
                for k in range(KC):
                    ins = tr(yz_ps[YZ[("XT",)]][:, k * TQ:(k + 1) * TQ], xq_norm[:, k * P:(k + 1) * P],
                             ident[0:TQ, 0:TQ])
                ins.then_inc(q_filled, 1)

            def q_part(b):
                pe.wait_ge(q_drained, b * 2 + 1)
                for m in range(KC):
                    ins = full(yz_ps[YZ[("Q",)]][:, m * TQ:(m + 1) * TQ],
                               lambda k: wq[:, k, m * P:(m + 1) * P], lambda k: xqT[:, k, :], KC)
                ins.then_inc(q_filled, 1)

            def tail_part(n, p):
                def need(who, name):
                    tail_wait(pe, who, name, p)

                x_free()
                if n == "o_turned":
                    pe.wait_ge(o_copied, p * 2 + 2)
                    for g in range(4):
                        ins = tr(x_ps[:, g * P:(g + 1) * P], o_sb[:, g, :], ident[:])
                elif n in ("on_turned", "at_turned", "ln2_turned", "ln3_turned"):
                    need("dve", {"on": "on", "at": "at", "ln2": "xn2", "ln3": "xn3"}[n.split("_")[0]])
                    src = xn if n[0:2] == "ln" else on
                    for k in range(KC):
                        ins = tr(x_ps[:, k * P:(k + 1) * P], src[:, k * P:(k + 1) * P], ident[:])
                elif n in ("cross_out", "self_out"):
                    need("act", "onT1" if n == "cross_out" else "atT")
                    w = wo if n == "cross_out" else so
                    ins = full(x_ps[:, 0:C], lambda k: tT[:, k, :], lambda k: w[:, k, :], KC)
                elif n == "qk":
                    need("dve", "xnT2")
                    for j, w in enumerate((sq, sk)):
                        for m in range(KC):
                            ins = full(x_ps[:, (KC * j + m) * P:(KC * j + m + 1) * P],
                                       lambda k: w[:, k, m * P:(m + 1) * P], lambda k: xnT[:, k, :], KC)
                elif n == "v":
                    for bb in range(2):
                        for half in range(2):
                            ins = full(x_ps[half * TQ:(half + 1) * TQ, bb * C:(bb + 1) * C],
                                       lambda k: xnT[:, k, bb * TQ:(bb + 1) * TQ],
                                       lambda k: sv[:, k, :], KC)
                elif n in ("s0", "s1"):
                    m = int(n[1])
                    need("dve", "kb11")
                    for bb in range(2):
                        ins = mm(x_ps[bb * TQ:(bb + 1) * TQ, :], sqT[:, m, bb * TQ:(bb + 1) * TQ],
                                 k_block[:, bb, m].rearrange("p h t -> p (h t)"), start=True, stop=True)
                elif n in ("p_turned0", "p_turned1"):
                    need("act", "p")
                    flat = s_sb[:].rearrange("p h t -> p (h t)")
                    for j in range(4):
                        q = 4 * int(n[-1]) + j
                        ins = tr(x_ps[:, j * P:(j + 1) * P], flat[:, q * P:(q + 1) * P], ident[:])
                elif n == "pv":
                    need("act", "pT1")
                    for bb in range(2):
                        for q in range(PAIRS):
                            ins = mm(x_ps[bb * TQ:(bb + 1) * TQ, q * 2 * D:(q + 1) * 2 * D],
                                     pT[:, q, bb * TQ:(bb + 1) * TQ], v_block[:, bb, q].rearrange("p h d -> p (h d)"),
                                     start=True, stop=True)
                elif n == "router":
                    need("dve", "xnT3")
                    ins = full(x_ps[:, 0:E], lambda k: xnT[:, k, :], lambda k: w_router[:, k, :], KC)
                elif n == "cumsum":
                    need("dve", "mask")
                    mm(x_ps[:, 0:E], tri[:], gate[:, 6, :], start=True, stop=False)
                    ins = mm(x_ps[:, 0:E], ones[:], chosen_before[:], start=False, stop=True)
                elif n == "hidden":
                    for m in range(KH):
                        ins = full(x_ps[:, m * P:(m + 1) * P], lambda k: w_gate[:, k, m * P:(m + 1) * P],
                                   lambda k: xnT[:, k, :], KC)
                elif n.startswith("down"):
                    need("dve", "hid")
                    j = int(n[4])
                    ins = full(x_ps[:], lambda k: hidden[:, k, :],
                               lambda k: w_down[:, k, j * 512:(j + 1) * 512], KH)
                ins.then_inc(t_pe, 1)
                last_x[0] = lambda: tail_wait(pe, *T_DRAIN[n], p)

            def begin():
                pe.wait_ge(consts_ready, N_CONST)
                pe.wait_ge(split_ready, N_SPLIT)
                pe.wait_ge(weights_in, 16 * N_WEIGHTS)

            def step(pe, b, c, i, main, prep, qprep, tail):
                if main and c == 0:
                    last_x[0] = lambda: pe.wait_ge(v_copied, b * V_USES + V_USES)
                    if isinstance(b, int) and b == 0:
                        pe.wait_ge(tail_weights_in, 16 * N_TAIL_WEIGHTS)
                for t, it in pieces():
                    if it in (S0, S1) and main:
                        scores(b, c, t, (S0, S1).index(it))
                    elif it[0] == "V" and prep:
                        v_part(b + 1, it[1])
                    elif it[0] == "K" and prep:
                        yz_free(it, b)
                        k_part(b + 1, it[1], it[2])
                    elif it[0] == "A" and prep:
                        yz_free(it, b)
                        a_part(b + 1, 1 - c, it[1], it[2])
                    elif it[0] == "XT" and qprep:
                        yz_free(it, b)
                        xt_part(b + 2)
                    elif it[0] == "Q" and qprep:
                        yz_free(it, b)
                        q_part(b + 2)
                    elif it == PV and main and t:
                        pv(b, c, t - 1)
                    elif it == T and tail:
                        for n in tail_of_slot(c, t):
                            tail_part(n, i - 1)
                if main:
                    pv(b, c, TILES - 1)

            def tail_only(p):
                for n in T_PE:
                    tail_part(n, p)

            run(pe, step, tail_only, begin)


def kernel(**inputs):
    import numpy as np
    import concourse.bacc as bacc
    from concourse.bass_utils import run_bass_kernel_spmd as run

    def turned(w):
        return np.ascontiguousarray(np.swapaxes(w, -1, -2))

    def columns(v):
        return np.ascontiguousarray(v.reshape(KC, P).T)

    x = inputs
    arrays = {
        "x": np.ascontiguousarray(x["x"]),
        "ctx_t": turned(x["ctx_1024"]).reshape(B * C, S),
        "wq": turned(x["L0_xattn_Wq"]), "wk": turned(x["L0_xattn_Wk"]),
        "wv": turned(x["L0_xattn_Wv"]), "wo": turned(x["L0_xattn_Wo"]),
        "bq": columns(x["L0_xattn_bq"]), "bk": columns(x["L0_xattn_bk"]),
        "bv": columns(x["L0_xattn_bv"]), "bo": np.ascontiguousarray(x["L0_xattn_bo"]),
        "sq": np.ascontiguousarray(x["L0_attn_Wq"]), "sk": np.ascontiguousarray(x["L0_attn_Wk"]),
        "sv": np.ascontiguousarray(x["L0_attn_Wv"]), "so": np.ascontiguousarray(x["L0_attn_Wo"]),
        "router": turned(x["L0_ffn_w_router"]), "gate": turned(x["L0_ffn_w_gate"]),
        "down": np.ascontiguousarray(x["L0_ffn_w_down"].transpose(2, 0, 1).reshape(HID, E * C)),
    }
    nc = bacc.Bacc("TRN2", target_bir_lowering=False, num_devices=1, dynamic_dma_scratch_size=256)
    aps = {n: nc.dram_tensor(f"in_{n}", v.shape, F32, kind="ExternalInput").ap() for n, v in arrays.items()}
    out = nc.dram_tensor("out", (B, TQ, C), F32, kind="ExternalOutput").ap()
    build(nc, aps, out)
    r = run(nc, [{f"in_{n}": v for n, v in arrays.items()}], core_ids=[0])
    return r.results[0]["out"]
```

```python
from contextlib import ExitStack

import concourse.bass as bass
from concourse import mybir

F32 = mybir.dt.float32
F32R = mybir.dt.float32r
U32 = mybir.dt.uint32
ALU = mybir.AluOpType
ACT = mybir.ActivationFunctionType
AX = mybir.AxisListType

P = 128
B, TQ, C = 32, 64, 256
S = 1601
H, D = 16, 16
KC = C // P
HM = P // D
HB = HM // 2
HR = P // 2
TILES = -(-S // P)
TAIL_ROWS = S - (TILES - 1) * P
GROUP = 4
GROUPS = -(-TILES // GROUP)
SP = S + 1
VW = D + 1
PAIRS = H // 2
BP = B // 2
E, TOPK, HID = 8, 2, 512
CAPACITY = -(-(B * TQ) * 5 // (E * 4))
KH = HID // P
EPS = 1e-5
GATE_EPS = 1e-6
NEG = -1e30
SCALE = D ** -0.5
HALF_SCALE = D ** -0.25

V_USES = -(-TILES // 2)
A_USES = 8 * (GROUPS - 1) + 2

S0, S1, PV, T = ("S0",), ("S1",), ("PV",), ("T",)
D0, D1, D2 = (("D", n) for n in range(3))


def k_(g, m):
    return ("K", g, m)


def v_(u):
    return ("V", u)


def a_(g, j):
    return ("A", g, j)


SLOTS = [
    [k_(0, 0), S0, S1, D0, PV, k_(0, 1), D1, D2, T],
    [S0, a_(0, 0), D0, S1, a_(0, 1), D1, v_(0), PV, a_(0, 2), D2, T],
    [S0, a_(0, 3), D0, S1, a_(0, 4), D1, v_(1), PV, a_(0, 5), D2, T],
    [a_(0, 6), k_(1, 0), S0, S1, D0, a_(0, 7), D1, PV, k_(1, 1), D2, T],
    [S0, a_(1, 0), D0, S1, a_(1, 1), D1, v_(2), PV, a_(1, 2), D2, T],
    [S0, a_(1, 3), D0, S1, a_(1, 4), D1, v_(3), PV, a_(1, 5), D2, T],
    [a_(1, 6), k_(2, 0), S0, S1, D0, a_(1, 7), D1, PV, k_(2, 1), D2, T],
    [S0, a_(2, 0), D0, S1, a_(2, 1), D1, v_(4), PV, a_(2, 2), D2, T],
    [S0, a_(2, 3), D0, S1, a_(2, 4), D1, v_(5), PV, a_(2, 5), D2, T],
    [a_(2, 6), k_(3, 0), S0, S1, D0, a_(2, 7), D1, PV, k_(3, 1), D2, T],
    [S0, a_(3, 0), D0, S1, a_(3, 1), D1, v_(6), PV, D2, T],
    [S0, ("M", 0), D0, S1, ("M", 1), D1, PV, ("XT",), D2, T],
    [S0, D0, S1, PV, D1, ("Q",), D2, T],
]

YZ_ORDER = [it for slot in SLOTS for it in slot if it[0] in ("K", "A", "M", "XT", "Q")]
YZ = {it: n % 2 for n, it in enumerate(YZ_ORDER)}
assert len(YZ_ORDER) % 2 == 0

T_PE = ["o_turned", "on_turned", "cross_out", "ln2_turned", "qk", "v", "s0", "s1", "p_turned0",
        "p_turned1", "pv", "at_turned", "self_out", "ln3_turned", "router", "cumsum", "hidden",
        "down0", "down1", "down2", "down3"]
T_DVE = ["rden", "on", "xbo", "x1", "stat2", "aggr2", "eps2", "xn2", "xnT2", "s0", "s1",
         "smax", "pT0", "ssum", "srec", "at", "x2", "stat3", "aggr3", "eps3", "xn3", "xnT3",
         "lmax", "esum", "erec", "gates", "top8", "topi", "topf",
         "oh0", "oh1", "mask", "keep", "msum", "kept", "gk", "gsum", "geps", "grec", "comb",
         "den", "sig0", "sig1", "sig2", "sig3", "y0", "y1", "y2", "y3", "y4", "y5", "y6", "y7"]
T_ACT = ["onT0", "onT1", "qkT", "vb0", "vb1", "p", "pT1", "atT", "gexp", "hexp", "hcopy"]
T_POOL = ["rstd2", "kb00", "kb01", "kb10", "kb11", "ssub", "rstd3", "hid"]
T_SLOT = dict(zip(T_PE, [0, 1, 2, 3, 4, 5, 6, 7, 9, 10, 11, 12, 13, 14, 15, 17, 18, 21, 22, 23, 24]))
PUT_OFF = {"xbo": ("o_turned", 1, 2), "xn2": ("cross_out", 1, 0), "p": ("s1", 2, 1),
           "ssum": ("p_turned0", 1, 0),
           "xn3": ("self_out", 1, 0), "gates": ("router", 1, 1), "sig0": ("hidden", 1, 1),
           "sig1": ("hidden", 1, 2), "sig2": ("hidden", 2, 1), "sig3": ("hidden", 2, 2),
           "hid": ("hidden", 3, 0)}
T_DRAIN = {
    "o_turned": ("dve", "on"), "on_turned": ("act", "onT1"), "cross_out": ("dve", "x1"),
    "ln2_turned": ("dve", "xnT2"), "qk": ("act", "qkT"), "v": ("act", "vb1"), "s0": ("dve", "s0"),
    "s1": ("dve", "s1"), "p_turned0": ("dve", "pT0"), "p_turned1": ("act", "pT1"),
    "pv": ("dve", "at"), "at_turned": ("act", "atT"), "self_out": ("dve", "x2"),
    "ln3_turned": ("dve", "xnT3"), "router": ("act", "gexp"), "cumsum": ("dve", "keep"),
    "hidden": ("act", "hcopy"), "down0": ("dve", "y1"), "down1": ("dve", "y3"),
    "down2": ("dve", "y5"), "down3": ("dve", "y7"),
}


def rows_of(t):
    return P if t < TILES - 1 else TAIL_ROWS


def cols_of(g):
    return min(GROUP * P, SP - g * GROUP * P)


def build(nc, a, out):
    with ExitStack() as ctx:
        def sb(name, shape, dt=F32):
            return ctx.enter_context(nc.sbuf_tensor(name, shape, dt))

        def sem(name):
            return ctx.enter_context(nc.semaphore(name))

        ident = sb("ident", [P, P])
        ones = sb("ones", [P, P])
        tri = sb("tri", [P, P])
        head_mask = sb("head_mask", [P, HM])
        block_mask = sb("block_mask", [P, HB])
        half_mask = sb("half_mask", [P, 2])
        causal = sb("causal", [P, TQ])
        iota8 = sb("iota8", [P, E])
        neg_half = sb("neg_half", [P, 1])
        wq = sb("wq", [P, KC, C])
        wo = sb("wo", [P, KC, C])
        wk_hi, wk_lo = sb("wk_hi", [P, KC, C], F32R), sb("wk_lo", [P, KC, C], F32R)
        wv_hi, wv_lo = sb("wv_hi", [P, KC, C], F32R), sb("wv_lo", [P, KC, C], F32R)
        bq, bk, bv = sb("bq", [P, KC]), sb("bk", [P, KC]), sb("bv", [P, KC])
        bo = sb("bo", [P, C])
        sq, sk, sv, so = (sb(f"s{n}", [P, KC, C]) for n in "qkvo")
        w_router = sb("w_router", [P, KC, E])
        w_gate = sb("w_gate", [P, KC, HID])
        w_down = sb("w_down", [P, KH, E * C])
        ctx_raw = sb("ctx_raw", [P, KC, GROUP * P])
        ctx_hi = [sb(f"ctx_hi{n}", [P, KC, GROUP * P], F32R) for n in range(2)]
        ctx_lo = [sb(f"ctx_lo{n}", [P, KC, GROUP * P], F32R) for n in range(2)]
        k_hi = [sb(f"k_hi{n}", [P, KC, GROUP * P], F32R) for n in range(2)]
        k_lo = [sb(f"k_lo{n}", [P, KC, GROUP * P], F32R) for n in range(2)]
        k_pair = sb("k_pair", [P, KC, 2, SP], F32R)
        k_one = sb("k_one", [HR + 1, KC, 2, SP], F32R)
        q_pair = [sb(f"q_pair{n}", [P, KC, 2, HB * TQ], F32R) for n in range(2)]
        q_max = [sb(f"q_max{n}", [HR + 1, KC, 2, HB * TQ], F32R) for n in range(2)]
        v_sb = [sb(f"v_sb{n}", [P, TILES * H * VW + 2 * D]) for n in range(2)]
        probs = [sb(f"probs{n}", [P, H * TQ]) for n in range(2)]
        q_hi, q_lo = sb("q_hi", [P, KC, HB * TQ], F32R), sb("q_lo", [P, KC, HB * TQ], F32R)
        maxima = sb("maxima", [P, GROUPS, PAIRS])
        neg_max = sb("neg_max", [P, PAIRS])
        xq = sb("xq", [TQ, C])
        xq_stat = sb("xq_stat", [TQ, 6])
        xq_mv = sb("xq_mv", [TQ, 4])
        xqT = sb("xqT", [P, KC, TQ])
        qT = sb("qT", [P, KC, TQ])
        qT_hi, qT_lo = sb("qT_hi", [P, KC, TQ], F32R), sb("qT_lo", [P, KC, TQ])
        o_sb = sb("o_sb", [P, 4, 2 * TQ])
        x_res = sb("x_res", [P, C])
        x_bo = x_res
        rden = sb("rden", [P, H])
        attended = sb("attended", [P, 2, C])
        on = attended[:, 0]
        tT = attended[:, 1].rearrange("p (k t) -> p k t", t=P)
        sqkT = attended[:].rearrange("p j (k t) -> p j k t", t=P)
        x1 = sb("x1", [P, C])
        x2 = x_res
        t_stat, t_mv = sb("t_stat", [P, 6]), sb("t_mv", [P, 4])
        xn = sb("xn", [P, C])
        xnT = sb("xnT", [P, KC, P])
        k_block = sb("k_block", [P, 2, KC, HB, TQ])
        v_block = sb("v_block", [P, 2, PAIRS, 2, D])
        s_sb = sb("s_sb", [P, H, TQ])
        flat_block = k_block[:].rearrange("p b k h t -> p (b k h t)")
        pT = flat_block[:, 0:PAIRS * P].rearrange("p (q t) -> p q t", t=P)
        hexp = flat_block[:, 0:HID].rearrange("p (m t) -> p m t", t=P)
        hidden = flat_block[:, HID:2 * HID].rearrange("p (m t) -> p m t", t=P)
        s_max, s_sum, s_rec = sb("s_max", [P, H]), sb("s_sum", [P, H]), sb("s_rec", [P, H])
        gate = sb("gate", [P, 12, E])
        gcol = sb("gcol", [P, 8])
        top_i = sb("top_i", [P, E], U32)
        chosen_before = sb("chosen_before", [P, E])
        y_sb = xn

        s_ps = [ctx.enter_context(nc.psum_tensor(f"s_ps{n}", [P, 2, 512], F32)) for n in range(2)]
        o_ps = ctx.enter_context(nc.psum_tensor("o_ps", [P, 512], F32))
        x_ps = ctx.enter_context(nc.psum_tensor("x_ps", [P, 512], F32))
        yz_ps = [ctx.enter_context(nc.psum_tensor(f"yz_ps{n}", [P, 512], F32)) for n in range(2)]

        weights_in = sem("weights_in")
        tail_weights_in = sem("tail_weights_in")
        consts_ready = sem("consts_ready")
        split_ready = sem("split_ready")
        ones_set = sem("ones_set")
        ctx_in = sem("ctx_in")
        xq_in = sem("xq_in")
        res_in = sem("res_in")
        out_done = sem("out_done")
        wait_carrier = sem("wait_carrier")
        ctx_hi_made = sem("ctx_hi_made")
        ctx_cut = sem("ctx_cut")
        k_filled, k_hi_made, k_lo_made = sem("k_filled"), sem("k_hi_made"), sem("k_lo_made")
        v_filled, v_copied = sem("v_filled"), sem("v_copied")
        a_filled, a_reduced = sem("a_filled"), sem("a_reduced")
        neg_max_made = sem("neg_max_made")
        max_turned, max_rows_made = sem("max_turned"), sem("max_rows_made")
        k_in = [sem(f"k_in{n}") for n in range(GROUPS)]
        q_in = sem("q_in")
        q_filled, q_drained = sem("q_filled"), sem("q_drained")
        q_norm_step = sem("q_norm_step")
        q_rstd = sem("q_rstd")
        q_cut_step = sem("q_cut_step")
        scores_ready, probs_ready, pv_done = sem("scores_ready"), sem("probs_ready"), sem("pv_done")
        o_copied = sem("o_copied")
        first_half_done = sem("first_half_done")
        t_pe, t_dve, t_act, t_pool = sem("t_pe"), sem("t_dve"), sem("t_act"), sem("t_pool")

        def apart(eng):
            eng.sem_inc(wait_carrier, 1)

        def tail_wait(eng, who, name, p):
            s, names = {"pe": (t_pe, T_PE), "dve": (t_dve, T_DVE), "act": (t_act, T_ACT),
                        "pool": (t_pool, T_POOL)}[who]
            eng.wait_ge(s, p * len(names) + names.index(name) + 1)

        N_CONST, N_SPLIT, N_WEIGHTS, N_TAIL_WEIGHTS = 14, 4, 7, 11
        MOVES = 6 * 16

        block = ctx.enter_context(nc.Block())

        def run(eng, step, tail_only, begin):
            begin()
            step(eng, -2, 0, None, main=False, prep=False, qprep=True, tail=False)
            step(eng, -1, 1, None, main=False, prep=True, qprep=True, tail=False)
            step(eng, 0, 0, 0, main=True, prep=True, qprep=True, tail=False)
            step(eng, 1, 1, 0, main=True, prep=True, qprep=True, tail=False)
            with eng.Fori(1, BP - 1) as i:
                step(eng, i * 2, 0, i, main=True, prep=True, qprep=True, tail=True)
                step(eng, i * 2 + 1, 1, i, main=True, prep=True, qprep=True, tail=True)
            step(eng, B - 2, 0, BP - 1, main=True, prep=True, qprep=False, tail=True)
            step(eng, B - 1, 1, BP - 1, main=True, prep=False, qprep=False, tail=True)
            tail_only(BP - 1)

        def pieces():
            return [(t, it) for t in range(TILES) for it in SLOTS[t]]

        def tail_of_slot(c, t):
            return [n for n in T_PE if T_SLOT[n] == c * TILES + t]

        def put_off_to(c, t, j):
            return [n for n, (fill, late, k) in PUT_OFF.items()
                    if T_SLOT[fill] + late == c * TILES + t and k == j]

        def put_off_of(fill):
            return [n for n, (f, _, _) in PUT_OFF.items() if f == fill]

        xr = a["x"].rearrange("b t d -> (b t) d")
        outr = out.rearrange("b t d -> (b t) d")
        ctx_t = a["ctx_t"]

        @block.sync
        def _(sp):
            def begin():
                def load(dst, src):
                    sp.dma_start(dst, src).then_inc(weights_in, 16)
                sp.sem_inc(out_done, 16)
                load(wq[:], a["wq"].rearrange("(k p) n -> p k n", p=P))
                load(staged[0], a["wk"].rearrange("(k p) n -> p k n", p=P))
                load(staged[1], a["wv"].rearrange("(k p) n -> p k n", p=P))
                for dst, n in ((bq, "bq"), (bk, "bk"), (bv, "bv")):
                    load(dst[:], a[n])
                load(bo[:], a["bo"].partition_broadcast(P))

            def late_weights(part):
                small = [(wo, "wo"), (sq, "sq"), (sk, "sk"), (sv, "sv"), (so, "so"),
                         (w_router, "router"), (w_gate, "gate")]
                for dst, n in small[2 * part:2 * part + 2]:
                    sp.dma_start(dst[:], a[n].rearrange("(k p) n -> p k n", p=P)).then_inc(tail_weights_in, 16)
                sp.dma_start(w_down[:, part, :], a["down"][part * P:(part + 1) * P, :]).then_inc(tail_weights_in, 16)

            def step(sp, b, c, i, main, prep, qprep, tail):
                if qprep:
                    if main or prep:
                        sp.wait_ge(q_filled, b * 2 + 3)
                    sp.dma_start(xq[:], xr[bass.ds(b * TQ + 2 * TQ, TQ), :]).then_inc(xq_in, 16)
                if prep:
                    stack_q(sp, b + 1, 1 - c, main)
                    load_ctx(sp, b + 1, 3)
                    stack_k(sp, b + 1, 0, main)
                if main and isinstance(b, int) and b == 0:
                    late_weights(0)
                if qprep:
                    load_ctx(sp, b + 2, 0)
                if prep:
                    stack_k(sp, b + 1, 1, main)
                if main and isinstance(b, int) and b == 0:
                    late_weights(1)
                if qprep:
                    load_ctx(sp, b + 2, 1)
                if prep:
                    stack_k(sp, b + 1, 2, main)
                if main and isinstance(b, int) and b == 0:
                    late_weights(2)
                if qprep:
                    load_ctx(sp, b + 2, 2)
                if prep:
                    stack_k(sp, b + 1, 3, main)
                if main and isinstance(b, int) and b == 0:
                    late_weights(3)

            def move(sp, dst, src, done):
                sp.dma_start(dst.bitcast(F32), src.bitcast(F32)).then_inc(done, 16)

            def stack_q(sp, b, c, main):
                sp.wait_ge(q_cut_step, b * 4 + 4)
                apart(sp)
                if main and not (isinstance(b, int) and b == 1):
                    sp.wait_ge(scores_ready, b * TILES - TILES)
                for hf in range(2):
                    rows = slice(hf * HR, (hf + 1) * HR)
                    move(sp, q_pair[c][0:HR, :, hf], q_hi[rows], q_in)
                    move(sp, q_pair[c][HR:P, :, hf], q_hi[rows], q_in)
                    move(sp, q_max[c][0:HR, :, hf], q_lo[rows], q_in)

            def stack_k(sp, b, gr, main):
                n = min(GROUP * P, S - gr * GROUP * P)
                cols = slice(gr * GROUP * P, gr * GROUP * P + n)
                sp.wait_ge(k_lo_made, b * 8 + gr * 2 + 2)
                apart(sp)
                if main:
                    sp.wait_ge(scores_ready, b * TILES - TILES + min(GROUP * gr + GROUP, TILES))
                for hf in range(2):
                    rows = slice(hf * HR, (hf + 1) * HR)
                    move(sp, k_pair[0:HR, :, hf, cols], k_hi[gr % 2][rows, :, 0:n], k_in[gr])
                    move(sp, k_pair[HR:P, :, hf, cols], k_lo[gr % 2][rows, :, 0:n], k_in[gr])
                    move(sp, k_one[0:HR, :, hf, cols], k_hi[gr % 2][rows, :, 0:n], k_in[gr])

            def load_ctx(sp, b, gr):
                if not (isinstance(b, int) and b == 0 and gr == 0):
                    sp.wait_ge(ctx_cut, b * GROUPS + gr)
                n = min(GROUP * P, S - gr * GROUP * P)
                sp.dma_start(ctx_raw[:, :, 0:n],
                             ctx_t[bass.ds(b * C, C), gr * GROUP * P:gr * GROUP * P + n]
                             .rearrange("(k p) s -> p k s", p=P)).then_inc(ctx_in, 16)

            def tail_only(p):
                sp.wait_ge(out_done, 16 * BP + 16)

            staged = [hidden[:].rearrange("p (k x) n -> p k (x n)", k=KC),
                      hexp[:].rearrange("p (k x) n -> p k (x n)", k=KC)]
            run(sp, step, tail_only, begin)

        @block.gpsimd
        def _(pool):
            g = nc.gpsimd

            def begin():
                n = [0]

                def made(ins):
                    n[0] += 1
                    ins.then_inc(consts_ready, 1)
                    pool.wait_ge(consts_ready, n[0])

                made(g.memset(ones[:], 1.0))
                made(g.affine_select(out=ident[:], in_=ones[:], compare_op=ALU.is_equal, fill=0.0, base=0,
                                     pattern=[[-1, P]], channel_multiplier=1))
                made(g.affine_select(out=tri[:], in_=ones[:], compare_op=ALU.is_ge, fill=0.0, base=0,
                                     pattern=[[1, P]], channel_multiplier=-1))
                made(g.affine_select(out=head_mask[:], in_=ones[:, 0:HM], compare_op=ALU.is_ge, fill=0.0,
                                     base=0, pattern=[[-D, HM]], channel_multiplier=1))
                made(g.affine_select(out=head_mask[:], in_=head_mask[:], compare_op=ALU.is_ge, fill=0.0,
                                     base=D - 1, pattern=[[D, HM]], channel_multiplier=-1))
                made(g.tensor_tensor(block_mask[:], head_mask[:, 0:HB], head_mask[:, HB:HM], ALU.add))
                made(g.affine_select(out=half_mask[:], in_=ones[:, 0:2], compare_op=ALU.is_ge, fill=0.0,
                                     base=0, pattern=[[-TQ, 2]], channel_multiplier=1))
                made(g.affine_select(out=half_mask[:], in_=half_mask[:], compare_op=ALU.is_ge, fill=0.0,
                                     base=TQ - 1, pattern=[[TQ, 2]], channel_multiplier=-1))
                made(g.memset(causal[:], 0.0))
                for lo in (0, TQ):
                    made(g.affine_select(out=causal[lo:lo + TQ, :], in_=causal[lo:lo + TQ, :],
                                         compare_op=ALU.is_ge, fill=NEG, base=0, pattern=[[-1, TQ]],
                                         channel_multiplier=1))
                made(g.iota(iota8[:], pattern=[[1, E]], base=0, channel_multiplier=0,
                            allow_small_or_imprecise_dtypes=True))
                made(g.memset(neg_half[:], -0.5))
                made(g.memset(chosen_before[:], 0.0))

            def cut_q(b):
                v = b * 4
                pool.wait_ge(q_drained, b * 2 + 2)
                if not (isinstance(b, int) and b == 0):
                    pool.wait_ge(q_cut_step, v)
                    pool.wait_ge(q_in, b * MOVES)
                    pool.wait_ge(a_filled, b * A_USES)
                apart(pool)
                g.tensor_copy(qT_hi[:], qT[:]).then_inc(q_cut_step, 1)
                pool.wait_ge(q_cut_step, v + 1)
                spread(q_hi, qT_hi[:].bitcast(F32)).then_inc(q_cut_step, 1)
                g.tensor_tensor(qT_lo[:], qT[:], qT_hi[:].bitcast(F32), ALU.subtract).then_inc(q_cut_step, 1)
                pool.wait_ge(q_cut_step, v + 3)
                spread(q_lo, qT_lo[:]).then_inc(q_cut_step, 1)

            def spread(dst, src):
                shape = [P, KC, HB, TQ]
                mask = block_mask[:].unsqueeze(2).unsqueeze(1).to_broadcast(shape)
                return g.tensor_tensor(dst[:].rearrange("p k (h t) -> p k h t", t=TQ),
                                       src.unsqueeze(2).to_broadcast(shape), mask, ALU.mult)

            def cut_ctx(b, c, gr):
                n = cols_of(gr)
                pool.wait_ge(ctx_in, (b * GROUPS + gr + 1) * 16)
                if gr >= 2:
                    pool.wait_ge(v_filled, b * V_USES + 2 * gr - 2)
                elif not (isinstance(b, int) and b == 0):
                    pool.wait_ge(v_filled, b * V_USES - 1 + gr)
                src = ctx_raw[:, :, 0:n]
                hi, lo = ctx_hi[gr % 2][:, :, 0:n], ctx_lo[gr % 2][:, :, 0:n]
                apart(pool)
                g.tensor_copy(hi, src).then_inc(ctx_hi_made, 1)
                pool.wait_ge(ctx_hi_made, b * GROUPS + gr + 1)
                g.tensor_tensor(lo, src, hi.bitcast(F32), ALU.subtract).then_inc(ctx_cut, 1)

            def rstd(s, mv, p):
                g.tensor_tensor(mv[:, 3:4], mv[:, 2:3], neg_half[0:p, :], ALU.pow).then_inc(s, 1)

            def step(pool, b, c, i, main, prep, qprep, tail):
                if prep:
                    cut_q(b + 1)
                for t in range(TILES):
                    if prep and t in (3, 6):
                        cut_ctx(b + 1, 1 - c, t // 3 + 1)
                    if qprep and t == (10 if prep else 9):
                        pool.wait_ge(q_norm_step, b * 4 + 11)
                        rstd(q_rstd, xq_mv, TQ)
                    if qprep and t in (9, 11):
                        cut_ctx(b + 2, c, (t - 9) // 2)
                    if tail:
                        for j in range(3):
                            for n in put_off_to(c, t, j):
                                tail_deferred(n, i - 1)
                        for n in tail_of_slot(c, t):
                            tail_part(n, i - 1)

            def tail_deferred(n, p):
                if n == "hid":
                    tail_wait(pool, "act", "hcopy", p)
                    tail_wait(pool, "dve", "sig3", p)
                    g.tensor_tensor(hidden, hidden, hexp, ALU.mult).then_inc(t_pool, 1)

            def tail_part(n, p):
                if n in ("cross_out", "self_out"):
                    k = "2" if n == "cross_out" else "3"
                    tail_wait(pool, "dve", "eps" + k, p)
                    rstd(t_pool, t_mv, P)
                elif n == "qk":
                    tail_wait(pool, "act", "qkT", p)
                    shape = [P, HB, TQ]
                    for bb in range(2):
                        for m in range(KC):
                            src = sqkT[:, 1, m, bb * TQ:(bb + 1) * TQ]
                            g.tensor_tensor(k_block[:, bb, m], src.unsqueeze(1).to_broadcast(shape),
                                            block_mask[:].unsqueeze(2).to_broadcast(shape),
                                            ALU.mult).then_inc(t_pool, 1)
                elif n == "s1":
                    tail_wait(pool, "dve", "smax", p)
                    g.tensor_tensor(s_sb[:], s_sb[:], s_max[:].unsqueeze(2).to_broadcast([P, H, TQ]),
                                    ALU.subtract).then_inc(t_pool, 1)

            def tail_only(p):
                for n in T_PE:
                    tail_part(n, p)
                    for d in put_off_of(n):
                        tail_deferred(d, p)

            run(pool, step, tail_only, begin)

        @block.scalar
        def _(act):
            s = nc.scalar

            def begin():
                act.wait_ge(consts_ready, N_CONST)
                for n in range(2):
                    s.activation(v_sb[n][:], ones[:, 0:1].to_broadcast(v_sb[n].shape),
                                 ACT.Copy).then_inc(ones_set, 1)
                s.activation(k_one[HR:HR + 1].rearrange("o m h s -> o (m h s)"),
                             ones[HR:HR + 1, 0:1].to_broadcast([1, KC * 2 * SP]),
                             ACT.Copy).then_inc(ones_set, 1)

            def load_res(act, p):
                act.dma_start(x_res[:], xr[bass.ds(p * P, P), :]).then_inc(res_in, 16)

            def store(act, p):
                tail_wait(act, "dve", "y7", p)
                act.dma_start(outr[bass.ds(p * P, P), :], y_sb[:]).then_inc(out_done, 16)

            def exp_tile(b, c, t):
                par, r = (c + t) % 2, rows_of(t)
                act.wait_ge(scores_ready, b * TILES + t + 1)
                if not (isinstance(b, int) and b == 0 and t < 2):
                    act.wait_ge(pv_done, b * TILES + t - 1)
                s.activation(probs[par][0:r, :], s_ps[par][0:r].rearrange("p a n -> p (a n)"),
                             ACT.Exp).then_inc(probs_ready, 1)

            def k_part(b, gr, m):
                n = cols_of(gr)
                if m == 0:
                    if gr >= 2:
                        act.wait_ge(k_in[gr - 2], b * MOVES + MOVES)
                    elif not (isinstance(b, int) and b == 0):
                        act.wait_ge(k_in[gr + 2], b * MOVES)
                act.wait_ge(k_filled, b * 8 + gr * 2 + m + 1)
                s.activation(k_hi[gr % 2][:, m, 0:n],
                             yz_ps[YZ[("K", gr, m)]][:, 0:n], ACT.Identity,
                             bias=bk[:, m:m + 1]).then_inc(k_hi_made, 1)

            def max_part(b, c, m):
                act.wait_ge(max_turned, b * 2 + m + 1)
                s.activation(q_max[c][HR:HR + 1, m].rearrange("o h n -> o (h n)"),
                             yz_ps[YZ[("M", m)]][HR:HR + 1, :], ACT.Copy).then_inc(max_rows_made, 1)

            def v_part(b, c, u):
                act.wait_ge(v_filled, b * V_USES + u + 1)
                n = 2 if 2 * u + 1 < TILES else 1
                r = rows_of(2 * u)
                dst = v_sb[c][0:r, 2 * u * H * VW:(2 * u + n) * H * VW].rearrange("p (h d) -> p h d", d=VW)
                src = x_ps[0:r, 0:n * C].rearrange("p (h d) -> p h d", d=D)
                s.activation(dst[:, :, 0:D], src, ACT.Copy).then_inc(v_copied, 1)

            def tail_deferred(n, p):
                if n == "p":
                    tail_wait(act, "pool", "ssub", p)
                    s.activation(s_sb[:], s_sb[:], ACT.Exp).then_inc(t_act, 1)

            def tail_part(n, p):
                if n not in ("on_turned", "qk", "v", "p_turned1", "at_turned", "router", "hidden"):
                    return
                tail_wait(act, "pe", n, p)
                if n == "on_turned":
                    for k in range(KC):
                        s.activation(tT[:, k, :], x_ps[:, k * P:(k + 1) * P], ACT.Identity,
                                     bias=bv[:, k:k + 1]).then_inc(t_act, 1)
                elif n == "qk":
                    s.activation(sqkT[:].rearrange("p j k t -> p (j k t)"), x_ps[:], ACT.Copy,
                                 scale=HALF_SCALE).then_inc(t_act, 1)
                elif n == "v":
                    src = x_ps[:].rearrange("p (b q h d) -> p (b q) h d", b=2, q=PAIRS, h=2)
                    for h in range(2):
                        dst = v_block[:].rearrange("p b q h d -> p (b q) h d")
                        s.activation(dst[:, :, h, :], src[:, :, h, :], ACT.Copy,
                                     scale=half_mask[:, h:h + 1]).then_inc(t_act, 1)
                elif n == "p_turned1":
                    s.activation(pT[:, 4:8, :], x_ps[:].rearrange("p (q t) -> p q t", q=4),
                                 ACT.Copy).then_inc(t_act, 1)
                elif n == "at_turned":
                    s.activation(tT[:], x_ps[:, 0:KC * P].rearrange("p (k t) -> p k t", k=KC),
                                 ACT.Copy).then_inc(t_act, 1)
                elif n == "router":
                    tail_wait(act, "dve", "lmax", p)
                    s.activation(gate[:, 0, :], x_ps[:, 0:E], ACT.Exp, bias=gcol[:, 0:1]).then_inc(t_act, 1)
                elif n == "hidden":
                    s.activation(hexp[:].rearrange("p m t -> p (m t)"), x_ps[:], ACT.Exp,
                                 scale=-1.0).then_inc(t_act, 1)
                    s.activation(hidden[:].rearrange("p m t -> p (m t)"), x_ps[:],
                                 ACT.Copy).then_inc(t_act, 1)

            def step(act, b, c, i, main, prep, qprep, tail):
                if not main and not prep:
                    act.wait_ge(weights_in, 16 * N_WEIGHTS)
                for t, it in pieces():
                    if it == S1 and main:
                        exp_tile(b, c, t)
                    elif it[0] == "K" and prep:
                        k_part(b + 1, it[1], it[2])
                    elif it[0] == "M" and prep:
                        max_part(b + 1, 1 - c, it[1])
                    elif it[0] == "V" and prep:
                        if it[1] == 0 and not main:
                            act.wait_ge(ones_set, 3)
                        v_part(b + 1, 1 - c, it[1])
                    elif it == T and t == TILES - 1 and c == 1 and main:
                        if tail:
                            store(act, i - 1)
                        load_res(act, i)
                    elif it[0] == "D" and tail:
                        for n in put_off_to(c, t, it[1]):
                            tail_deferred(n, i - 1)
                    elif it == T and tail:
                        for n in tail_of_slot(c, t):
                            tail_part(n, i - 1)

            def tail_only(p):
                for n in T_PE:
                    tail_part(n, p)
                    for d in put_off_of(n):
                        tail_deferred(d, p)
                store(act, p)

            run(act, step, tail_only, begin)

        @block.vector
        def _(dve):
            v = nc.vector

            def begin():
                n = [0]

                def made(ins):
                    n[0] += 1
                    ins.then_inc(split_ready, 1)
                    dve.wait_ge(split_ready, n[0])

                dve.wait_ge(consts_ready, N_CONST)
                dve.wait_ge(weights_in, 16 * N_WEIGHTS)
                for src, hi, lo in ((hidden, wk_hi, wk_lo), (hexp, wv_hi, wv_lo)):
                    src = src[:].rearrange("p (k x) n -> p k (x n)", k=KC)
                    made(v.tensor_copy(hi[:], src))
                    made(v.tensor_tensor(lo[:], src, hi[:].bitcast(F32), ALU.subtract))

            def k_part(b, gr, m):
                n = cols_of(gr)
                dve.wait_ge(k_hi_made, b * 8 + gr * 2 + m + 1)
                v.scalar_tensor_tensor(out=k_lo[gr % 2][:, m, 0:n], in0=yz_ps[YZ[("K", gr, m)]][:, 0:n],
                                       scalar=bk[:, m:m + 1], in1=k_hi[gr % 2][:, m, 0:n].bitcast(F32),
                                       op0=ALU.add, op1=ALU.subtract).then_inc(k_lo_made, 1)

            def a_part(b, c, gr, j):
                n = 8 * gr + j
                dve.wait_ge(a_filled, b * A_USES + n + 1)
                ps = yz_ps[YZ[("A", gr, j)]]
                if gr < GROUPS - 1:
                    v.tensor_reduce(maxima[:, gr, j:j + 1], ps[:, 0:GROUP * P], AX.X,
                                    ALU.max).then_inc(a_reduced, 1)
                else:
                    w = cols_of(gr)
                    src = ps[:, 0:4 * w].rearrange("p (m k n) -> p m k n", m=KC, k=2)[:, :, :, 0:TAIL_ROWS]
                    dst = maxima[:, gr].rearrange("p (m h k) -> p m h k", m=KC, k=2)[:, :, j, :]
                    v.tensor_reduce(dst, src, AX.X,
                                    ALU.max).then_inc(a_reduced, 1)

            def max_part(b):
                dve.wait_ge(a_reduced, b * A_USES + A_USES)
                v.tensor_reduce(neg_max[:], maxima[:].rearrange("p g q -> p q g"), AX.X, ALU.max,
                                negate=True).then_inc(neg_max_made, 1)

            def norm_stats(b):
                dve.wait_ge(xq_in, b * 16 + 16)
                v.bn_stats(xq_stat[:], xq[:]).then_inc(q_norm_step, 1)
                dve.wait_ge(q_norm_step, b * 4 + 1)
                apart(dve)
                v.bn_aggr(xq_mv[:, 0:2], xq_stat[:]).then_inc(q_norm_step, 1)
                dve.wait_ge(q_norm_step, b * 4 + 2)
                v.tensor_scalar(xq_mv[:, 2:3], xq_mv[:, 1:2], EPS, None, ALU.add).then_inc(q_norm_step, 1)

            def norm_apply(b):
                dve.wait_ge(q_rstd, b + 1)
                v.tensor_scalar(xq[:], xq[:], xq_mv[:, 0:1], xq_mv[:, 3:4], ALU.subtract,
                                ALU.mult).then_inc(q_norm_step, 1)

            def xt_part(b):
                dve.wait_ge(q_filled, b * 2 + 1)
                v.tensor_copy(xqT[:].rearrange("p k t -> p (k t)"),
                              yz_ps[YZ[("XT",)]][:, 0:KC * TQ]).then_inc(q_drained, 1)

            def q_part(b):
                dve.wait_ge(q_filled, b * 2 + 2)
                if not (isinstance(b, int) and b == 0):
                    dve.wait_ge(q_cut_step, b * 4)
                for m in range(KC):
                    ins = v.tensor_scalar(qT[:, m, :], yz_ps[YZ[("Q",)]][:, m * TQ:(m + 1) * TQ],
                                          bq[:, m:m + 1], SCALE, ALU.add, ALU.mult)
                ins.then_inc(q_drained, 1)

            def copy_o(b, c, i):
                dve.wait_ge(pv_done, b * TILES + TILES)
                src = o_ps[:, 0:4 * TQ].rearrange("p (g t) -> p g t", g=4)
                v.tensor_copy(o_sb[:, :, c * TQ:(c + 1) * TQ], src).then_inc(o_copied, 1)

            def bcast(ap, shape, axis):
                return ap.unsqueeze(axis).to_broadcast(shape)

            def counted(p):
                def done(ins, name):
                    ins.then_inc(t_dve, 1)
                    tail_wait(dve, "dve", name, p)
                return done

            def tail_deferred(n, p):
                done = counted(p)
                if n == "xbo":
                    dve.wait_ge(res_in, p * 16 + 16)
                    done(v.tensor_tensor(x_bo[:], x_res[:], bo[:], ALU.add), n)
                elif n in ("xn2", "xn3"):
                    k, x = n[2], (x1 if n == "xn2" else x2)
                    tail_wait(dve, "pool", "rstd" + k, p)
                    done(v.tensor_scalar(xn[:], x[:], t_mv[:, 0:1], t_mv[:, 3:4], ALU.subtract, ALU.mult),
                         "xn" + k)
                elif n == "ssum":
                    tail_wait(dve, "act", "p", p)
                    done(v.tensor_reduce(s_sum[:], s_sb[:], AX.X, ALU.add), "ssum")
                    done(v.reciprocal(s_rec[:], s_sum[:]), "srec")
                elif n == "gates":
                    tail_wait(dve, "act", "gexp", p)
                    done(v.tensor_reduce(gcol[:, 1:2], gate[:, 0, :], AX.X, ALU.add), "esum")
                    done(v.reciprocal(gcol[:, 2:3], gcol[:, 1:2]), "erec")
                    done(v.tensor_scalar(gate[:, 1, :], gate[:, 0, :], gcol[:, 2:3], None, ALU.mult), "gates")
                    apart(dve)
                    done(v.max(gate[:, 2, :], gate[:, 1, :]), "top8")
                    apart(dve)
                    done(v.max_index(top_i[:], gate[:, 2, :], gate[:, 1, :]), "topi")
                    done(v.tensor_copy(gate[:, 3, :], top_i[:]), "topf")
                    for k in range(TOPK):
                        done(v.tensor_scalar(gate[:, 4 + k, :], iota8[:], gate[:, 3, k:k + 1], None,
                                             ALU.is_equal), f"oh{k}")
                    done(v.tensor_tensor(gate[:, 6, :], gate[:, 4, :], gate[:, 5, :], ALU.add), "mask")
                elif n.startswith("sig"):
                    if n == "sig0":
                        tail_wait(dve, "act", "hexp", p)
                        done(v.tensor_scalar(hexp, hexp, 1.0, None, ALU.add), "den")
                    m = int(n[3])
                    done(v.reciprocal(hexp[:, m, :], hexp[:, m, :]), n)

            def tail_part(n, p):
                done = counted(p)

                def norm(x, k):
                    done(v.bn_stats(t_stat[:], x[:]), "stat" + k)
                    apart(dve)
                    done(v.bn_aggr(t_mv[:, 0:2], t_stat[:]), "aggr" + k)
                    done(v.tensor_scalar(t_mv[:, 2:3], t_mv[:, 1:2], EPS, None, ALU.add), "eps" + k)

                if n not in ("on_turned", "qk", "v", "p_turned1", "at_turned", "hidden"):
                    tail_wait(dve, "pe", n, p)
                if n == "o_turned":
                    o = x_ps[:].rearrange("p (h d) -> p h d", d=2 * D)
                    done(v.reciprocal(rden[:].unsqueeze(2), o[:, :, D:D + 1]), "rden")
                    done(v.tensor_tensor(on[:].rearrange("p (h d) -> p h d", d=D), o[:, :, 0:D],
                                         bcast(rden[:], [P, H, D], 2), ALU.mult), "on")
                elif n == "cross_out":
                    done(v.tensor_tensor(x1[:], x_ps[:, 0:C], x_bo[:], ALU.add), "x1")
                    dve.wait_ge(out_done, p * 16 + 16)
                    norm(x1, "2")
                elif n in ("ln2_turned", "ln3_turned"):
                    done(v.tensor_copy(xnT[:].rearrange("p k t -> p (k t)"), x_ps[:, 0:KC * P]),
                         "xnT" + n[2])
                elif n in ("s0", "s1"):
                    m = int(n[1])
                    done(v.tensor_tensor(s_sb[:, m * HM:(m + 1) * HM, :],
                                         x_ps[:].rearrange("p (h t) -> p h t", t=TQ),
                                         bcast(causal[:], [P, HM, TQ], 1), ALU.add), n)
                    if m == 1:
                        done(v.tensor_reduce(s_max[:], s_sb[:], AX.X, ALU.max), "smax")
                elif n == "p_turned0":
                    done(v.tensor_copy(pT[:, 0:4, :], x_ps[:].rearrange("p (q t) -> p q t", q=4)), "pT0")
                elif n == "pv":
                    done(v.tensor_tensor(on[:].rearrange("p (h d) -> p h d", d=D),
                                         x_ps[:, 0:C].rearrange("p (h d) -> p h d", d=D),
                                         bcast(s_rec[:], [P, H, D], 2), ALU.mult), "at")
                elif n == "self_out":
                    done(v.tensor_tensor(x2[:], x_ps[:, 0:C], x1[:], ALU.add), "x2")
                    norm(x2, "3")
                elif n == "router":
                    done(v.tensor_reduce(gcol[:, 0:1], x_ps[:, 0:E], AX.X, ALU.max, negate=True), "lmax")
                elif n == "cumsum":
                    done(v.tensor_scalar(gate[:, 7, :], x_ps[:, 0:E], float(CAPACITY), None, ALU.is_le),
                         "keep")
                    done(v.tensor_tensor(chosen_before[:], chosen_before[:], gate[:, 6, :], ALU.add), "msum")
                    done(v.tensor_tensor(gate[:, 8, :], gate[:, 6, :], gate[:, 7, :], ALU.mult), "kept")
                    done(v.tensor_tensor(gate[:, 9, :], gate[:, 8, :], gate[:, 1, :], ALU.mult), "gk")
                    done(v.tensor_reduce(gcol[:, 3:4], gate[:, 9, :], AX.X, ALU.add), "gsum")
                    done(v.tensor_scalar(gcol[:, 4:5], gcol[:, 3:4], GATE_EPS, None, ALU.add), "geps")
                    done(v.reciprocal(gcol[:, 5:6], gcol[:, 4:5]), "grec")
                    done(v.tensor_scalar(gate[:, 10, :], gate[:, 9, :], gcol[:, 5:6], None, ALU.mult), "comb")
                elif n.startswith("down"):
                    for k in range(2):
                        e = 2 * int(n[4]) + k
                        done(v.scalar_tensor_tensor(out=y_sb[:], in0=x_ps[:, k * C:(k + 1) * C],
                                                    scalar=gate[:, 10, e:e + 1],
                                                    in1=(x2 if e == 0 else y_sb)[:], op0=ALU.mult,
                                                    op1=ALU.add), f"y{e}")

            def step(dve, b, c, i, main, prep, qprep, tail):
                for t, it in pieces():
                    if it[0] == "K" and prep:
                        k_part(b + 1, it[1], it[2])
                    elif it[0] == "A" and prep:
                        a_part(b + 1, 1 - c, it[1], it[2])
                        if it == a_(GROUPS - 1, 1):
                            max_part(b + 1)
                    elif it == PV and qprep and t == 9:
                        norm_stats(b + 2)
                    elif it == PV and qprep and t == 10:
                        norm_apply(b + 2)
                    elif it[0] == "XT" and qprep:
                        xt_part(b + 2)
                    elif it[0] == "Q" and qprep:
                        q_part(b + 2)
                    elif it[0] == "D" and tail:
                        for n in put_off_to(c, t, it[1]):
                            tail_deferred(n, i - 1)
                    elif it == T and tail:
                        for n in tail_of_slot(c, t):
                            tail_part(n, i - 1)
                if main:
                    if c == 0 and not (isinstance(i, int) and i == 0):
                        tail_wait(dve, "pe", "o_turned", i - 1)
                    copy_o(b, c, i)

            def tail_only(p):
                for n in T_PE:
                    tail_part(n, p)
                    for d in put_off_of(n):
                        tail_deferred(d, p)

            run(dve, step, tail_only, begin)

        @block.tensor
        def _(pe):
            mm, tr = nc.tensor.matmul, nc.tensor.transpose
            last_x = [None]

            def x_free():
                if last_x[0] is not None:
                    last_x[0]()

            def yz_free(it, b):
                n = YZ_ORDER.index(it)
                if isinstance(b, int) and b == -2:
                    return
                if n < 2:
                    pe.wait_ge(q_drained, b * 2 + n + 3)
                elif YZ_ORDER[n - 2][0] == "M":
                    pe.wait_ge(max_rows_made, b * 2 + YZ_ORDER[n - 2][1] + 3)
                elif YZ_ORDER[n - 2][0] == "K":
                    _, gr, m = YZ_ORDER[n - 2]
                    pe.wait_ge(k_lo_made, b * 8 + gr * 2 + m + 9)
                else:
                    _, gr, j = YZ_ORDER[n - 2]
                    pe.wait_ge(a_reduced, b * A_USES + A_USES + gr * 8 + j + 1)

            def three(out_, wt_hi, wt_lo, mv_hi, mv_lo):
                n = 0
                for k in range(KC):
                    for w_, m_ in ((wt_hi, mv_hi), (wt_hi, mv_lo), (wt_lo, mv_hi)):
                        ins = mm(out_, w_[:, k], m_[:, k], start=(n == 0), stop=(n == 3 * KC - 1))
                        n += 1
                return ins

            def full(out_, w_, m_, chunks):
                for k in range(chunks):
                    ins = mm(out_, w_(k), m_(k), start=(k == 0), stop=(k == chunks - 1))
                return ins

            def k_part(b, gr, m):
                n, cols = cols_of(gr), slice(m * P, (m + 1) * P)
                if m == 0:
                    pe.wait_ge(ctx_cut, b * GROUPS + gr + 1)
                ch, cl = ctx_hi[gr % 2][:, :, 0:n], ctx_lo[gr % 2][:, :, 0:n]
                three(yz_ps[YZ[("K", gr, m)]][:, 0:n], wk_hi[:, :, cols], wk_lo[:, :, cols], ch,
                      cl).then_inc(k_filled, 1)

            def v_part(b, u):
                x_free()
                for t in range(2 * u, min(2 * u + 2, TILES)):
                    gr, r = t // GROUP, rows_of(t)
                    cols = slice((t % GROUP) * P, (t % GROUP) * P + r)
                    ins = three(x_ps[0:r, (t % 2) * C:(t % 2 + 1) * C], ctx_hi[gr % 2][:, :, cols],
                                ctx_lo[gr % 2][:, :, cols], wv_hi[:], wv_lo[:])
                ins.then_inc(v_filled, 1)
                last_x[0] = lambda: pe.wait_ge(v_copied, b * V_USES + u + 1)

            def a_part(b, gr, j):
                if gr == 0 and j == 0:
                    pe.wait_ge(q_cut_step, b * 4 + 2)
                if gr == GROUPS - 1 and j == 0:
                    pe.wait_ge(k_hi_made, b * 8 + gr * 2 + 2)
                elif gr < GROUPS - 1 and j % 4 == 0:
                    pe.wait_ge(k_hi_made, b * 8 + gr * 2 + j // 4 + 1)
                n = cols_of(gr)
                ps = yz_ps[YZ[("A", gr, j)]]
                pairs = [j] if gr < GROUPS - 1 else [4 * m + 2 * j + k for m in range(KC) for k in range(2)]
                for k, q in enumerate(pairs):
                    m, rows = q // 4, slice(q % 4 // 2 * HR, q % 4 // 2 * HR + HR)
                    ins = mm(ps[:, k * n:(k + 1) * n], q_hi[rows, m, (q % 2) * P:(q % 2 + 1) * P],
                             k_hi[gr % 2][rows, m, 0:n], start=True, stop=True)
                ins.then_inc(a_filled, 1)

            def scores(b, c, t, m):
                par, r = (c + t) % 2, rows_of(t)
                if m == 0:
                    if t == 0:
                        pe.wait_ge(q_in, b * MOVES + MOVES)
                        pe.wait_ge(max_rows_made, b * 2 + 2)
                    if t % GROUP == 0:
                        pe.wait_ge(k_in[t // GROUP], b * MOVES + MOVES)
                    if not (isinstance(b, int) and b == 0 and t < 2):
                        pe.wait_ge(probs_ready, b * TILES + t - 1)
                cols = slice(t * P, t * P + r)
                for hf in range(2):
                    o = s_ps[par][0:r, m, hf * HB * TQ:(hf + 1) * HB * TQ]
                    mm(o, k_pair[:, m, hf, cols], q_pair[c][:, m, hf], start=True, stop=False)
                    ins = mm(o, k_one[:, m, hf, cols], q_max[c][:, m, hf], start=False, stop=True)
                if m == KC - 1:
                    ins.then_inc(scores_ready, 1)

            def pv(b, c, t):
                par, r = (c + t) % 2, rows_of(t)
                pe.wait_ge(probs_ready, b * TILES + t + 1)
                if t == 0:
                    pe.wait_ge(v_copied, b * V_USES + V_USES)
                    if not (isinstance(b, int) and b == 0):
                        pe.wait_ge(o_copied, b)
                for gr in range(4):
                    for j in range(4):
                        h = 4 * gr + j
                        off = (t * H + h) * VW
                        ins = mm(o_ps[32 * j:32 * j + 32, gr * TQ:(gr + 1) * TQ],
                                 v_sb[c][0:r, off:off + 32], probs[par][0:r, h * TQ:(h + 1) * TQ],
                                 start=(t == 0 and gr == 0), stop=(t == TILES - 1 and gr == 3),
                                 skip_group_check=True)
                ins.then_inc(pv_done, 1)

            def max_turn(b, m):
                pe.wait_ge(neg_max_made, b + 1)
                for j in range(4):
                    q = 4 * m + j
                    ins = mm(yz_ps[YZ[("M", m)]][HR:HR + 1, j * P:(j + 1) * P], neg_max[:, q:q + 1],
                             ident[:], start=True, stop=True)
                ins.then_inc(max_turned, 1)

            def xt_part(b):
                pe.wait_ge(q_norm_step, b * 4 + 4)
                apart(pe)
                for k in range(KC):
                    ins = tr(yz_ps[YZ[("XT",)]][:, k * TQ:(k + 1) * TQ], xq[:, k * P:(k + 1) * P],
                             ident[0:TQ, 0:TQ])
                ins.then_inc(q_filled, 1)

            def q_part(b):
                pe.wait_ge(q_drained, b * 2 + 1)
                for m in range(KC):
                    ins = full(yz_ps[YZ[("Q",)]][:, m * TQ:(m + 1) * TQ],
                               lambda k: wq[:, k, m * P:(m + 1) * P], lambda k: xqT[:, k, :], KC)
                ins.then_inc(q_filled, 1)

            def tail_part(n, p):
                def need(who, name):
                    tail_wait(pe, who, name, p)

                x_free()
                if n == "o_turned":
                    pe.wait_ge(o_copied, p * 2 + 2)
                    for g in range(4):
                        ins = tr(x_ps[:, g * P:(g + 1) * P], o_sb[:, g, :], ident[:])
                elif n in ("on_turned", "at_turned", "ln2_turned", "ln3_turned"):
                    need("dve", {"on": "on", "at": "at", "ln2": "xn2", "ln3": "xn3"}[n.split("_")[0]])
                    src = xn if n[0:2] == "ln" else on
                    for k in range(KC):
                        ins = tr(x_ps[:, k * P:(k + 1) * P], src[:, k * P:(k + 1) * P], ident[:])
                elif n in ("cross_out", "self_out"):
                    need("act", "onT1" if n == "cross_out" else "atT")
                    w = wo if n == "cross_out" else so
                    ins = full(x_ps[:, 0:C], lambda k: tT[:, k, :], lambda k: w[:, k, :], KC)
                elif n == "qk":
                    need("dve", "xnT2")
                    for j, w in enumerate((sq, sk)):
                        for m in range(KC):
                            ins = full(x_ps[:, (KC * j + m) * P:(KC * j + m + 1) * P],
                                       lambda k: w[:, k, m * P:(m + 1) * P], lambda k: xnT[:, k, :], KC)
                elif n == "v":
                    for bb in range(2):
                        for half in range(2):
                            ins = full(x_ps[half * TQ:(half + 1) * TQ, bb * C:(bb + 1) * C],
                                       lambda k: xnT[:, k, bb * TQ:(bb + 1) * TQ],
                                       lambda k: sv[:, k, :], KC)
                elif n in ("s0", "s1"):
                    m = int(n[1])
                    need("pool", "kb11")
                    apart(pe)
                    for hf in range(2):
                        rows = slice(hf * HR, (hf + 1) * HR)
                        for bb in range(2):
                            ins = mm(x_ps[bb * TQ:(bb + 1) * TQ, hf * HB * TQ:(hf + 1) * HB * TQ],
                                     sqkT[rows, 0, m, bb * TQ:(bb + 1) * TQ],
                                     k_block[rows, bb, m].rearrange("p h t -> p (h t)"),
                                     start=True, stop=True)
                        if hf == 0:
                            ins.then_inc(first_half_done, 1)
                            pe.wait_ge(first_half_done, p * 2 + m + 1)
                            apart(pe)
                elif n in ("p_turned0", "p_turned1"):
                    need("act", "p")
                    flat = s_sb[:].rearrange("p h t -> p (h t)")
                    for j in range(4):
                        q = 4 * int(n[-1]) + j
                        ins = tr(x_ps[:, j * P:(j + 1) * P], flat[:, q * P:(q + 1) * P], ident[:])
                elif n == "pv":
                    need("act", "pT1")
                    for bb in range(2):
                        for q in range(PAIRS):
                            ins = mm(x_ps[bb * TQ:(bb + 1) * TQ, q * 2 * D:(q + 1) * 2 * D],
                                     pT[:, q, bb * TQ:(bb + 1) * TQ], v_block[:, bb, q].rearrange("p h d -> p (h d)"),
                                     start=True, stop=True)
                elif n == "router":
                    need("dve", "xnT3")
                    ins = full(x_ps[:, 0:E], lambda k: xnT[:, k, :], lambda k: w_router[:, k, :], KC)
                elif n == "cumsum":
                    need("dve", "mask")
                    mm(x_ps[:, 0:E], tri[:], gate[:, 6, :], start=True, stop=False)
                    ins = mm(x_ps[:, 0:E], ones[:], chosen_before[:], start=False, stop=True)
                elif n == "hidden":
                    for m in range(KH):
                        ins = full(x_ps[:, m * P:(m + 1) * P], lambda k: w_gate[:, k, m * P:(m + 1) * P],
                                   lambda k: xnT[:, k, :], KC)
                elif n.startswith("down"):
                    need("pool", "hid")
                    j = int(n[4])
                    ins = full(x_ps[:], lambda k: hidden[:, k, :],
                               lambda k: w_down[:, k, j * 512:(j + 1) * 512], KH)
                ins.then_inc(t_pe, 1)
                last_x[0] = lambda: tail_wait(pe, *T_DRAIN[n], p)

            def begin():
                pe.wait_ge(consts_ready, N_CONST)
                pe.wait_ge(split_ready, N_SPLIT)
                pe.wait_ge(weights_in, 16 * N_WEIGHTS)

            def step(pe, b, c, i, main, prep, qprep, tail):
                if main and c == 0:
                    last_x[0] = lambda: pe.wait_ge(v_copied, b * V_USES + V_USES)
                    if isinstance(b, int) and b == 0:
                        pe.wait_ge(ones_set, 3)
                for t, it in pieces():
                    if it in (S0, S1) and main:
                        scores(b, c, t, (S0, S1).index(it))
                    elif it[0] == "V" and prep:
                        v_part(b + 1, it[1])
                    elif it[0] == "K" and prep:
                        yz_free(it, b)
                        k_part(b + 1, it[1], it[2])
                    elif it[0] == "A" and prep:
                        yz_free(it, b)
                        a_part(b + 1, it[1], it[2])
                    elif it[0] == "M" and prep:
                        yz_free(it, b)
                        max_turn(b + 1, it[1])
                    elif it[0] == "XT" and qprep:
                        yz_free(it, b)
                        xt_part(b + 2)
                    elif it[0] == "Q" and qprep:
                        yz_free(it, b)
                        q_part(b + 2)
                    elif it == PV and main and t:
                        pv(b, c, t - 1)
                    elif it == T and tail:
                        for n in tail_of_slot(c, t):
                            tail_part(n, i - 1)
                if main:
                    pv(b, c, TILES - 1)
                if isinstance(b, int) and b == 1:
                    pe.wait_ge(tail_weights_in, 16 * N_TAIL_WEIGHTS)

            def tail_only(p):
                for n in T_PE:
                    tail_part(n, p)

            run(pe, step, tail_only, begin)


def kernel(**inputs):
    import numpy as np
    import concourse.bacc as bacc
    from concourse.bass_utils import run_bass_kernel_spmd as run

    def turned(w):
        return np.ascontiguousarray(np.swapaxes(w, -1, -2))

    def columns(v):
        return np.ascontiguousarray(v.reshape(KC, P).T)

    x = inputs
    arrays = {
        "x": np.ascontiguousarray(x["x"]),
        "ctx_t": turned(x["ctx_1024"]).reshape(B * C, S),
        "wq": turned(x["L0_xattn_Wq"]), "wk": turned(x["L0_xattn_Wk"]),
        "wv": turned(x["L0_xattn_Wv"]), "wo": turned(x["L0_xattn_Wo"]),
        "bq": columns(x["L0_xattn_bq"]), "bk": columns(x["L0_xattn_bk"]),
        "bv": columns(x["L0_xattn_bv"]), "bo": np.ascontiguousarray(x["L0_xattn_bo"]),
        "sq": np.ascontiguousarray(x["L0_attn_Wq"]), "sk": np.ascontiguousarray(x["L0_attn_Wk"]),
        "sv": np.ascontiguousarray(x["L0_attn_Wv"]), "so": np.ascontiguousarray(x["L0_attn_Wo"]),
        "router": turned(x["L0_ffn_w_router"]), "gate": turned(x["L0_ffn_w_gate"]),
        "down": np.ascontiguousarray(x["L0_ffn_w_down"].transpose(2, 0, 1).reshape(HID, E * C)),
    }
    nc = bacc.Bacc("TRN2", target_bir_lowering=False, num_devices=1, dynamic_dma_scratch_size=256)
    aps = {n: nc.dram_tensor(f"in_{n}", v.shape, F32, kind="ExternalInput").ap() for n, v in arrays.items()}
    out = nc.dram_tensor("out", (B, TQ, C), F32, kind="ExternalOutput").ap()
    build(nc, aps, out)
    r = run(nc, [{f"in_{n}": v for n, v in arrays.items()}], core_ids=[0])
    return r.results[0]["out"]
```
